# Optimizing a Trainium2 kernel written in Bass

```python
import numpy as np
import jax
import jax.numpy as jnp

def _softmax(x, axis=-1):
    return jax.nn.softmax(x, axis=axis)

def _gelu(x):
    return jax.nn.gelu(x, approximate=True)

def _silu(x):
    return jax.nn.silu(x)

def _sigmoid(x):
    return jax.nn.sigmoid(x)

def _layernorm(x, axis=-1, eps=1e-05):
    m = jnp.mean(x, axis=axis, keepdims=True)
    v = jnp.var(x, axis=axis, keepdims=True)
    return (x - m) / jnp.sqrt(v + eps)

def _scatter_add(tgt, idx, src, axis=0):
    return tgt.at[idx].add(src)

def _segment_sum(src, seg, n):
    return jax.ops.segment_sum(src, seg, n)
kernel_name = 'mk_cond_resid_d4_seqx_r8_7d1d31'

def setup_inputs(seed: int=0):
    np.random.seed(seed)
    _w = jnp.asarray

    def _rec_inputs():
        import jax
        import jax.numpy as jnp
        _rk = jax.random.key(seed)
        x = -0.0003929 + 0.9999 * jax.random.normal(jax.random.fold_in(_rk, 1), (32, 128, 128), jnp.float32)
        _lenS = 128 - jax.random.randint(jax.random.fold_in(_rk, 7), (32,), 0, max(1, 128 // 4) + 1, jnp.int32)
        _lenS2 = 128 - jax.random.randint(jax.random.fold_in(_rk, 8), (32,), 0, max(1, 128 // 4) + 1, jnp.int32)
        itok_B_0_7 = jax.random.randint(jax.random.fold_in(_rk, 11), (32,), 0, 8, jnp.int32)
        itok_B_0_2 = jax.random.randint(jax.random.fold_in(_rk, 12), (32,), 0, 3, jnp.int32)
        itok_B_0_6 = jax.random.randint(jax.random.fold_in(_rk, 13), (32,), 0, 7, jnp.int32)
        fside_BxSxS_0 = 4.13588e-05 + 0.999923 * jax.random.normal(jax.random.fold_in(_rk, 14), (32, 128, 128), jnp.float32)
        itok_B_0_5 = jax.random.randint(jax.random.fold_in(_rk, 15), (32,), 0, 6, jnp.int32)
        return (x, itok_B_0_7, itok_B_0_2, itok_B_0_6, fside_BxSxS_0, itok_B_0_5)
    x, itok_B_0_7, itok_B_0_2, itok_B_0_6, fside_BxSxS_0, itok_B_0_5 = _rec_inputs()

    def _L0_cond_setup():
        import jax, jax.numpy as jnp
        import numpy as np
        S, O, H = (8, 128, 128)
        B, N = (32, 64)
        key = jax.random.key(seed)
        k1, k2, k3, k4 = jax.random.split(key, 4)
        x = jax.random.normal(k1, (B, N, H), dtype=jnp.float32)
        subject_id = jax.random.randint(k2, (B,), 0, S)
        wbound = jnp.sqrt(2.0 / 6.0) * jnp.sqrt(3.0 / H)
        weight = jax.random.uniform(k3, (S, O, H), minval=-wbound, maxval=wbound, dtype=jnp.float32)
        bbound = 1.0 / jnp.sqrt(H)
        bias = jax.random.uniform(k4, (S, O), minval=-bbound, maxval=bbound, dtype=jnp.float32)
        return {'x': x, 'subject_id': subject_id, 'weight': weight, 'bias': bias}
    _L0_cond_all = _L0_cond_setup()
    _L0_cond_in = {k: v for k, v in _L0_cond_all.items() if k in ('weight', 'bias')}
    del _L0_cond_all

    def _L1_cond_setup():
        import jax, jax.numpy as jnp
        import numpy as np
        B, S, D, F, E = (8, 256, 128, 512, 5)

        def _dense(x, wi_, wo_):
            return jax.nn.relu(x @ wi_) @ wo_
        key = jax.random.key(seed)
        ks = jax.random.split(key, 9)
        sc = 0.02
        return {'hidden_states': jax.random.normal(ks[0], (B, S, D), jnp.float32), 'type_label': jax.random.randint(ks[1], (B,), 0, E, jnp.int32), 'wi': jax.random.normal(ks[2], (E, D, F), jnp.float32) * sc, 'wo': jax.random.normal(ks[3], (E, F, D), jnp.float32) * sc, 'swi': jax.random.normal(ks[4], (2, D, F), jnp.float32) * sc, 'swo': jax.random.normal(ks[5], (2, F, D), jnp.float32) * sc, 'g1': jax.random.normal(ks[6], (3 * D, D), jnp.float32) * sc, 'g2': jax.random.normal(ks[7], (D, 3), jnp.float32) * sc}
    _L1_cond_all = _L1_cond_setup()
    _L1_cond_in = {k: v for k, v in _L1_cond_all.items() if k in ('wi', 'wo', 'swi', 'swo', 'g1', 'g2')}
    del _L1_cond_all

    def _L2_cond_setup():
        import jax, jax.numpy as jnp
        import numpy as np
        N_PROFILES = 8
        HIDDEN = 128
        BOTTLENECK = 128
        EPS = 1e-05
        key = jax.random.key(seed)
        ks = jax.random.split(key, 8)
        B, S, H, K, P = (16, 256, HIDDEN, BOTTLENECK, N_PROFILES)
        down_w = jax.random.normal(ks[0], (P, H, K), dtype=jnp.float32) * (1.0 / np.sqrt(H))
        down_b = jax.random.normal(ks[1], (P, K), dtype=jnp.float32) * 0.01
        up_w = jax.random.normal(ks[2], (P, K, H), dtype=jnp.float32) * (1.0 / np.sqrt(K))
        up_b = jax.random.normal(ks[3], (P, H), dtype=jnp.float32) * 0.01
        ln_g = jnp.ones((P, H), dtype=jnp.float32)
        ln_b = jnp.zeros((P, H), dtype=jnp.float32)
        hidden = jax.random.normal(ks[4], (B, S, H), dtype=jnp.float32)
        profile_ids = jax.random.randint(ks[5], (B,), 0, P)
        return {'hidden': hidden, 'profile_ids': profile_ids, 'down_w': down_w, 'down_b': down_b, 'up_w': up_w, 'up_b': up_b, 'ln_g': ln_g, 'ln_b': ln_b}
    _L2_cond_all = _L2_cond_setup()
    _L2_cond_in = {k: v for k, v in _L2_cond_all.items() if k in ('down_w', 'down_b', 'up_w', 'up_b', 'ln_g', 'ln_b')}
    del _L2_cond_all

    def _L3_cond_setup():
        import jax, jax.numpy as jnp
        import numpy as np
        B, S, D = (8, 128, 128)
        NUM_STAGES = 6
        key = jax.random.key(seed)
        k1, k2, k3, k4, k5 = jax.random.split(key, 5)
        return {'query': jax.random.normal(k1, (B, S, D), dtype=jnp.float32), 'key': jax.random.normal(k2, (B, S, D), dtype=jnp.float32), 'value': jax.random.normal(k3, (B, S, D), dtype=jnp.float32), 'braak_embed': jax.random.normal(k4, (NUM_STAGES, D), dtype=jnp.float32), 'braak_stages': jax.random.randint(k5, (B,), 0, NUM_STAGES, dtype=jnp.int64)}
    _L3_cond_all = _L3_cond_setup()
    _L3_cond_in = {k: v for k, v in _L3_cond_all.items() if k in ('braak_embed',)}
    del _L3_cond_all
    return {'x': x, 'itok_B_0_7': itok_B_0_7, 'itok_B_0_2': itok_B_0_2, 'itok_B_0_6': itok_B_0_6, 'fside_BxSxS_0': fside_BxSxS_0, 'itok_B_0_5': itok_B_0_5, 'L0_cond_weight': _L0_cond_in['weight'], 'L0_cond_bias': _L0_cond_in['bias'], 'L1_cond_wi': _L1_cond_in['wi'], 'L1_cond_wo': _L1_cond_in['wo'], 'L1_cond_swi': _L1_cond_in['swi'], 'L1_cond_swo': _L1_cond_in['swo'], 'L1_cond_g1': _L1_cond_in['g1'], 'L1_cond_g2': _L1_cond_in['g2'], 'L2_cond_down_w': _L2_cond_in['down_w'], 'L2_cond_down_b': _L2_cond_in['down_b'], 'L2_cond_up_w': _L2_cond_in['up_w'], 'L2_cond_up_b': _L2_cond_in['up_b'], 'L2_cond_ln_g': _L2_cond_in['ln_g'], 'L2_cond_ln_b': _L2_cond_in['ln_b'], 'L3_cond_braak_embed': _L3_cond_in['braak_embed']}

def reference(x, itok_B_0_7, itok_B_0_2, itok_B_0_6, fside_BxSxS_0, itok_B_0_5, L0_cond_weight, L0_cond_bias, L1_cond_wi, L1_cond_wo, L1_cond_swi, L1_cond_swo, L1_cond_g1, L1_cond_g2, L2_cond_down_w, L2_cond_down_b, L2_cond_up_w, L2_cond_up_b, L2_cond_ln_g, L2_cond_ln_b, L3_cond_braak_embed):
    import jax
    import jax.numpy as jnp

    def _L0_cond_ref(x, subject_id, weight, bias):
        import jax, jax.numpy as jnp
        import numpy as np
        S, O, H = (8, 128, 128)
        B, N = (32, 64)
        W = weight[subject_id]
        b = bias[subject_id]
        y = jnp.einsum('bnh,boh->bno', x, W) + b[:, None, :]
        return y

    def _L1_cond_ref(hidden_states, type_label, wi, wo, swi, swo, g1, g2):
        import jax, jax.numpy as jnp
        import numpy as np
        B, S, D, F, E = (8, 256, 128, 512, 5)

        def _dense(x, wi_, wo_):
            return jax.nn.relu(x @ wi_) @ wo_
        x = hidden_states
        s0 = _dense(x, swi[0], swo[0])
        s1 = _dense(x, swi[1], swo[1])
        wi_sel = wi[type_label]
        wo_sel = wo[type_label]
        h = jax.nn.relu(jnp.einsum('bsd,bdf->bsf', x, wi_sel))
        eo = jnp.einsum('bsf,bfd->bsd', h, wo_sel)
        gate_in = jnp.concatenate([eo[:, 0], s0[:, 0], s1[:, 0]], axis=-1)
        w = jax.nn.softmax(jax.nn.relu(gate_in @ g1) @ g2, axis=-1)
        w = w[:, :, None, None]
        return eo * w[:, 0] + s0 * w[:, 1] + s1 * w[:, 2]

    def _L2_cond_ref(hidden, profile_ids, down_w, down_b, up_w, up_b, ln_g, ln_b):
        import jax, jax.numpy as jnp
        import numpy as np
        N_PROFILES = 8
        HIDDEN = 128
        BOTTLENECK = 128
        EPS = 1e-05
        Wd = down_w[profile_ids]
        bd = down_b[profile_ids][:, None]
        Wu = up_w[profile_ids]
        bu = up_b[profile_ids][:, None]
        g = ln_g[profile_ids][:, None]
        b = ln_b[profile_ids][:, None]
        z = jax.nn.relu(jnp.einsum('bsh,bhk->bsk', hidden, Wd) + bd)
        y = hidden + jnp.einsum('bsk,bkh->bsh', z, Wu) + bu
        mu = jnp.mean(y, axis=-1, keepdims=True)
        var = jnp.mean(jnp.square(y - mu), axis=-1, keepdims=True)
        return (y - mu) * jax.lax.rsqrt(var + EPS) * g + b

    def _L3_cond_ref(query, key, value, braak_embed, braak_stages):
        import jax, jax.numpy as jnp
        import numpy as np
        B, S, D = (8, 128, 128)
        NUM_STAGES = 6
        bias = braak_embed[braak_stages][..., None]
        q = query + bias
        attn = jnp.einsum('bsd,btd->bst', q, key)
        attn = jax.nn.softmax(attn, axis=-1)
        return jnp.einsum('bst,btd->bsd', attn, value)
    x = x + _L0_cond_ref(x, itok_B_0_7, L0_cond_weight, L0_cond_bias)
    x = x + _L1_cond_ref(x, itok_B_0_2, L1_cond_wi, L1_cond_wo, L1_cond_swi, L1_cond_swo, L1_cond_g1, L1_cond_g2)
    x = x + _L2_cond_ref(x, itok_B_0_6, L2_cond_down_w, L2_cond_down_b, L2_cond_up_w, L2_cond_up_b, L2_cond_ln_g, L2_cond_ln_b)
    x = x + _L3_cond_ref(x, fside_BxSxS_0, fside_BxSxS_0, L3_cond_braak_embed, itok_B_0_5)
    return x

_drawn_inputs = setup_inputs


def setup_inputs(seed=0):
    import zlib

    import numpy as np

    out = dict(_drawn_inputs(seed))
    spreads = {'L2_cond_ln_g': (1.0, 0.2), 'L2_cond_ln_b': (0.0, 0.1)}
    factors = {'L1_cond_g1': 8.0, 'L1_cond_g2': 8.0, 'L2_cond_down_b': 8.0, 'L2_cond_up_b': 8.0}
    for name, (base, spread) in spreads.items():
        noise = np.random.default_rng([zlib.crc32(name.encode()), seed]).standard_normal(out[name].shape)
        drawn = base * np.exp(spread * noise) if base else spread * noise
        out[name] = jnp.asarray(drawn.astype(out[name].dtype))
    for name, factor in factors.items():
        out[name] = (out[name] * factor).astype(out[name].dtype)
    return out
```

```python
from contextlib import ExitStack

import concourse.bass as bass
from concourse import mybir

F32 = mybir.dt.float32
F32R = mybir.dt.float32r
I32 = mybir.dt.int32
ALU = mybir.AluOpType
ACT = mybir.ActivationFunctionType
AX = mybir.AxisListType

GB = 4
UNITS = 12
NSH = 8
EPS = 1e-5
RSQRT_MAGIC = float(0x5F3759DF)
NEWTON = 3
HEAD = 1
LN_STEPS = 3 + 3 * NEWTON
WRAP_FIRST, WRAP_LAST = 2, 7


def after(eng, sem, count):
    if isinstance(count, int) and count <= 0:
        return
    eng.wait_ge(sem, count)


class Slot:

    def __init__(self, i, p, h, prep, mlp, prev, attn):
        self.i, self.p, self.h = i, p, h
        self.prep = prep
        self.mlp = mlp
        self.prev = prev
        self.attn = attn


def run_slots(eng, body, before_slot=None):
    for i, flags in ((-1, (1, 0, 0, 0)), (0, (1, 1, 0, 0)), (1, (1, 1, 1, 0))):
        if before_slot:
            before_slot(i)
        body(Slot(i, i % 2, i // 2, *flags))
    with eng.Fori(WRAP_FIRST // 2, (WRAP_LAST + 1) // 2) as pair:
        for p in range(2):
            body(Slot(pair * 2 + p, p, pair, 1, 1, 1, 1))
    body(Slot(8, 0, 4, 0, 0, 1, 1))
    body(Slot(9, 1, 4, 0, 0, 0, 1))


def build(nc, x, id7, id2, id6, side, id5, w0, b0, wi, wo, swi, swo, g1, g2,
          down_w, down_b, up_w, up_b, ln_g, ln_b, embed, out):
    B, N, D = x.shape
    E, _, F = wi.shape
    P0, P2, P3 = w0.shape[0], down_w.shape[0], embed.shape[0]
    FC = F // D
    W = GB * N
    NG = B // GB
    RAW = F + FC * D
    assert N == D == 128 and W == 512 and FC == 4 and NG == 8

    with ExitStack() as ctx:
        def sb(name, shape, dt=F32):
            return ctx.enter_context(nc.sbuf_tensor(name, shape, dt))

        def sem(name):
            return ctx.enter_context(nc.semaphore(name))

        shared = sb("shared", [128, 2, 2, RAW], F32R)
        experts = sb("experts", [128, E, 2, RAW], F32R)
        w0_table = sb("w0_table", [128, P0, 128])
        ln_table = sb("ln_table", [128, 3, P2, 128])
        columns = sb("columns", [128, 3, B])
        g1_sb = sb("g1_sb", [128, 3, 128])
        g2_sb = sb("g2_sb", [128, 3])
        ident = sb("ident", [128, 128])
        ones = sb("ones", [128, 128])
        ids = sb("ids", [1, 4, B], I32)
        stage = sb("stage", [128, 2, RAW])
        w0_raw = sb("w0_raw", [128, P0, 128])
        ids_rows = sb("ids_rows", [P0, 3, B], I32)
        row_i = sb("row_i", [P0, 1], I32)
        row_f = sb("row_f", [P0, 1])
        onehot = sb("onehot", [P0, 3, B])
        bias_rows = sb("bias_rows", [P0, 3, 128])
        esel = sb("esel", [128, GB, 2, RAW], F32R)
        w0_sel = sb("w0_sel", [128, GB, 128])
        wd_sel = sb("wd_sel", [128, GB, 128])
        wu_sel = sb("wu_sel", [128, GB, 128])
        b0_sel = sb("b0_sel", [128, GB])
        bd_sel = sb("bd_sel", [128, GB])
        em_sel = sb("em_sel", [128, GB])
        xin = sb("xin", [128, 2, GB, 128])
        keys = sb("keys", [128, 2, GB, 128])
        xT = sb("xT", [128, W])
        x1T = sb("x1T", [128, 2, W])
        x1h = sb("x1h", [128, 2, W], F32R)
        x1l = sb("x1l", [128, 2, W], F32R)
        hid_hi = sb("hid_hi", [128, 4, W], F32R)
        hid_lo = sb("hid_lo", [128, 4, W], F32R)
        acc_sb = sb("acc_sb", [128, 2, 3, W])
        gprod = sb("gprod", [128, GB, 3])
        gmax = sb("gmax", [128, GB])
        gsub = sb("gsub", [128, GB, 3])
        gexp = sb("gexp", [128, GB, 3])
        gsum = sb("gsum", [128, GB])
        grec = sb("grec", [128, GB])
        gate = sb("gate", [128, GB, 3])
        x2T = sb("x2T", [128, W])
        x2n = sb("x2n", [128, W])
        x2b = sb("x2b", [128, W])
        zT = sb("zT", [128, W])
        y = sb("y", [128, W])
        stats = sb("stats", [128, GB, 6])
        meanvar = sb("meanvar", [128, GB, 2])
        var = sb("var", [128, GB])
        half = sb("half", [128, GB], I32)
        rstd = sb("rstd", [128, GB])
        nt = sb("nt", [128, 2, GB])
        yn = sb("yn", [128, W])
        yg = sb("yg", [128, W])
        x3 = sb("x3", [128, W])
        xq = sb("xq", [128, W])
        qT = sb("qT", [128, W])
        kT = sb("kT", [128, W])
        negmax = sb("negmax", [128, GB])
        probs = sb("probs", [128, W])
        psums = sb("psums", [128, GB])
        prec = sb("prec", [128, GB])
        pT = sb("pT", [128, W])
        o_sb = sb("o_sb", [128, W])

        hid_ps = [ctx.enter_context(nc.psum_tensor(f"hid_ps{n}", [128, W], F32)) for n in range(3)]
        acc_ps = [ctx.enter_context(nc.psum_tensor(f"acc_ps{n}", [128, W], F32)) for n in range(3)]
        misc = [ctx.enter_context(nc.psum_tensor(f"misc{n}", [128, W], F32)) for n in range(2)]

        ids_in = sem("ids_in")
        idrows_in = sem("idrows_in")
        w0_in = sem("w0_in")
        gates_in = sem("gates_in")
        lntab_in = sem("lntab_in")
        stage_in = [sem("stage_in0"), sem("stage_in1")]
        consts = sem("consts")
        w0t_done = sem("w0t_done")
        w0tab_ready = sem("w0tab_ready")
        rowf_ready = sem("rowf_ready")
        onehot_ready = sem("onehot_ready")
        cols_done = sem("cols_done")
        cols_ready = sem("cols_ready")
        tab_hi = sem("tab_hi")
        tab_lo = sem("tab_lo")
        x_in = [sem("x_in0"), sem("x_in1")]
        k_in = [sem("k_in0"), sem("k_in1")]
        w0_sel_in = sem("w0_sel_in")
        l2w_in = sem("l2w_in")
        esel_in = [sem(f"esel_in{b}") for b in range(GB)]
        stored = sem("stored")
        hid_done = sem("hid_done")
        out_done = sem("out_done")
        kt_done, xt_done, g1_done, x3t_done = sem("kt_done"), sem("xt_done"), sem("g1_done"), sem("x3t_done")
        g2_done, qk_done, l0_done, pt_done = sem("g2_done"), sem("qk_done"), sem("l0_done"), sem("pt_done")
        x2n_done, z_done, pv_done, y_done = sem("x2n_done"), sem("z_done"), sem("pv_done"), sem("y_done")
        hi_ready = sem("hi_ready")
        acc_ready = sem("acc_ready")
        kt_ready, xt_ready, qt_ready = sem("kt_ready"), sem("xt_ready"), sem("qt_ready")
        gexp_ready, probs_ready, x1h_ready = sem("gexp_ready"), sem("probs_ready"), sem("x1h_ready")
        pt_ready, x2n_ready, zt_ready = sem("pt_ready"), sem("x2n_ready"), sem("zt_ready")
        lo_ready = sem("lo_ready")
        gprod_ready, gmax_ready, gsub_ready = sem("gprod_ready"), sem("gmax_ready"), sem("gsub_ready")
        gate_steps, mixed = sem("gate_steps"), sem("mixed")
        negmax_ready, x1_ready, prec_ready = sem("negmax_ready"), sem("x1_ready"), sem("prec_ready")
        o_ready, y_ready = sem("o_ready"), sem("y_ready")
        stats_ready, meanvar_ready = sem("stats_ready"), sem("meanvar_ready")
        ln_steps, yn_ready = sem("ln_steps"), sem("yn_ready")
        b0_sel_ready, bd_sel_ready, em_sel_ready = sem("b0_sel_ready"), sem("bd_sel_ready"), sem("em_sel_ready")
        yg_steps, x3_ready, xq_ready = sem("yg_steps"), sem("x3_ready"), sem("xq_ready")
        x1l_ready, x2b_ready = sem("x1l_ready"), sem("x2b_ready")

        block = ctx.enter_context(nc.Block())

        def cols(t, b):
            return t[:, b * 128:(b + 1) * 128]

        TABLES = [(shared[:, e], swi[e], swo[e]) for e in range(2)] + \
                 [(experts[:, e], wi[e], wo[e]) for e in range(E)]

        @block.sync
        def _(sp):
            sp.sem_inc(stored, 16 * HEAD)
            for n, t in enumerate((id7, id2, id6, id5)):
                sp.dma_start(ids[0:1, n, :], t.rearrange("(a b) -> a b", a=1)).then_inc(ids_in, 16)
            sp.dma_start(w0_raw[:, :, :], w0.rearrange("s o h -> o s h")).then_inc(w0_in, 16)

            def load_x(g, p):
                first = (g * GB) % B
                sp.dma_start(xin[:, p], x[bass.ds(first, GB)].rearrange("b n d -> n b d")).then_inc(x_in[p], 16)

            def load_w0(g):
                for b in range(GB):
                    who = sp.value_load(ids[0:1, 0, bass.ds((g * GB + b) % B, 1)], min_val=0, max_val=P0 - 1)
                    sp.dma_start(w0_sel[:, b, :], w0_table[:, bass.ds(who, 1), :]).then_inc(w0_sel_in, 16)

            def load_stage(n):
                if n >= 2:
                    sp.wait_ge(tab_lo, n - 1)
                sp.dma_start(stage[:, n % 2, 0:F], TABLES[n][1]).then_inc(stage_in[n % 2], 16)
                sp.dma_start(stage[:, n % 2, F:RAW].rearrange("p (c d) -> p c d", c=FC),
                             TABLES[n][2].rearrange("(c p) d -> p c d", p=128)).then_inc(stage_in[n % 2], 16)

            load_x(0, 0)
            for n, (t, rows) in enumerate(((id7, P0), (id6, P2), (id5, P3))):
                sp.dma_start(ids_rows[0:rows, n, :], t.partition_broadcast(rows)).then_inc(idrows_in, 16)
            for n, (t, rows) in enumerate(((b0, P0), (down_b, P2), (embed, P3))):
                sp.dma_start(bias_rows[0:rows, n, :], t).then_inc(idrows_in, 16)
            load_stage(0)
            load_stage(1)
            sp.wait_ge(ids_in, 64)
            sp.wait_ge(w0tab_ready, 2)
            load_w0(0)
            for n, t in enumerate((up_b, ln_g, ln_b)):
                sp.dma_start(ln_table[:, n], t.partition_broadcast(128)).then_inc(lntab_in, 16)
            sp.dma_start(g1_sb[:, :, :], g1.rearrange("(c p) j -> p c j", p=128)).then_inc(gates_in, 16)
            sp.dma_start(g2_sb[:, :], g2).then_inc(gates_in, 16)
            for n in range(2, 2 + E):
                load_stage(n)

            def slot(s):
                i, p, h = s.i, s.p, s.h
                if s.prev:
                    after(sp, y_done, i - 1)
                    for b in range(GB):
                        who = sp.value_load(ids[0:1, 2, bass.ds(i * GB - GB + b, 1)], min_val=0, max_val=P2 - 1)
                        sp.dma_start(wd_sel[:, b, :], down_w[bass.ds(who, 1)].rearrange("s h k -> (s h) k")).then_inc(l2w_in, 16)
                        sp.dma_start(wu_sel[:, b, :], up_w[bass.ds(who, 1)].rearrange("s k h -> (s k) h")).then_inc(l2w_in, 16)
                if s.mlp:
                    for b in range(GB):
                        after(sp, out_done, i * UNITS - GB + b + 1)
                        who = sp.value_load(ids[0:1, 1, bass.ds(i * GB + b, 1)], min_val=0, max_val=E - 1)
                        sp.dma_start(esel[:, b].rearrange("p t f -> p (t f)").bitcast(F32),
                                     experts[:, bass.ds(who, 1)].rearrange("p e t f -> p (e t f)").bitcast(F32)).then_inc(esel_in[b], 16)
                if s.prev:
                    after(sp, pv_done, i - 2 + HEAD)
                    sp.dma_start(keys[:, 1 - p], side[bass.ds(i * GB - GB, GB)].rearrange("b n d -> n b d")).then_inc(k_in[1 - p], 16)
                if s.prep:
                    after(sp, xt_done, i + 1)
                    load_x(i + 2, p)
                    after(sp, l0_done, i + 2)
                    load_w0(i + 2)
                if s.attn:
                    after(sp, o_ready, i - 1 + HEAD)
                    sp.dma_start(out[bass.ds(i * GB - 2 * GB, GB)].rearrange("b n d -> n b d"),
                                 o_sb[:, :].rearrange("n (b d) -> n b d", b=GB)).then_inc(stored, 16)

            def tables_first(i):
                if i == 0:
                    sp.wait_ge(tab_lo, 2 + E)

            run_slots(sp, slot, tables_first)
            sp.wait_ge(x_in[0], 16 * (NG // 2 + 1))
            sp.wait_ge(x_in[1], 16 * (NG // 2 + 1))
            sp.wait_ge(w0_sel_in, 16 * GB * (NG + 2))
            sp.wait_ge(stored, 16 * (NG + HEAD))

        @block.tensor
        def _(pe):
            for s_ in (qk_done, x3t_done, pv_done,):
                pe.sem_inc(s_, HEAD)
            def transposes(bank, src, done):
                for b in range(GB):
                    mm = pe.transpose(cols(bank, b), src(b), ident[:, :])
                mm.then_inc(done, 1)

            pe.wait_ge(consts, 3)
            pe.wait_ge(w0_in, 16)
            for half_ in range(2):
                transposes(misc[half_], lambda b: w0_raw[:, half_ * GB + b, :], w0t_done)
            pe.wait_ge(idrows_in, 96)
            pe.wait_ge(onehot_ready, 1)
            for n, rows in enumerate((P0, P2, P3)):
                mm = pe.matmul(hid_ps[0][:, n * B:(n + 1) * B], bias_rows[0:rows, n, :], onehot[0:rows, n, :],
                               start=True, stop=True)
            mm.then_inc(cols_done, 1)
            pe.wait_ge(w0tab_ready, 2)

            def hidden(k, s):
                i, p = s.i, s.p
                bank = hid_ps[k % 3]
                if k == 0:
                    pe.wait_ge(x1h_ready, i + 1)
                    pe.wait_ge(x1l_ready, i + 1)
                    if isinstance(i, int) and i == 0:
                        pe.wait_ge(cols_ready, 1)
                after(pe, lo_ready, i * UNITS + k - 2)
                if k < NSH:
                    e, c = k // FC, k % FC
                    if isinstance(i, int) and i == 0 and c == 0:
                        pe.wait_ge(tab_lo, e + 1)
                    w_hi, w_lo = cols(shared[:, e, 0], c), cols(shared[:, e, 1], c)
                    pe.matmul(bank[:, :], w_hi, x1h[:, p], start=True, stop=False)
                    pe.matmul(bank[:, :], w_lo, x1h[:, p], start=False, stop=False)
                    mm = pe.matmul(bank[:, :], w_hi, x1l[:, p], start=False, stop=True)
                else:
                    b = k - NSH
                    pe.wait_ge(esel_in[b], i * 16 + 16)
                    xh, xl = cols(x1h[:, p], b), cols(x1l[:, p], b)
                    for c in range(FC):
                        w_hi, w_lo = cols(esel[:, b, 0], c), cols(esel[:, b, 1], c)
                        pe.matmul(cols(bank, c), w_hi, xh, start=True, stop=False)
                        pe.matmul(cols(bank, c), w_lo, xh, start=False, stop=False)
                        mm = pe.matmul(cols(bank, c), w_hi, xl, start=False, stop=True)
                mm.then_inc(hid_done, 1)

            def output(k, i):
                pe.wait_ge(lo_ready, i * UNITS + k + 1)
                h_hi, h_lo = hid_hi[:, k % 4], hid_lo[:, k % 4]
                if k < NSH:
                    e, c = k // FC, k % FC
                    if c == 0:
                        after(pe, acc_ready, i * 3 - 2 + e)
                    w_hi, w_lo = cols(shared[:, e, 0], FC + c), cols(shared[:, e, 1], FC + c)
                    pe.matmul(acc_ps[e][:, :], w_hi, h_hi, start=(c == 0), stop=False)
                    pe.matmul(acc_ps[e][:, :], w_lo, h_hi, start=False, stop=False)
                    mm = pe.matmul(acc_ps[e][:, :], w_hi, h_lo, start=False, stop=(c == FC - 1))
                else:
                    b = k - NSH
                    if b == 0:
                        after(pe, acc_ready, i * 3)
                    o = cols(acc_ps[2], b)
                    for c in range(FC):
                        w_hi, w_lo = cols(esel[:, b, 0], FC + c), cols(esel[:, b, 1], FC + c)
                        pe.matmul(o, w_hi, cols(h_hi, c), start=(c == 0), stop=False)
                        pe.matmul(o, w_lo, cols(h_hi, c), start=False, stop=False)
                        mm = pe.matmul(o, w_hi, cols(h_lo, c), start=False, stop=(c == FC - 1))
                mm.then_inc(out_done, 1)

            def piece(t, s):
                i, p, h = s.i, s.p, s.h
                bank = misc[t % 2]
                if t == 0 and s.attn:
                    pe.wait_ge(k_in[p], h * 16)
                    after(pe, o_ready, i - 2 + HEAD)
                    transposes(bank, lambda b: keys[:, p, b, :], kt_done)
                if t == 1 and s.prep:
                    pe.wait_ge(x_in[1 - p], (h + 1 + p) * 16)
                    after(pe, y_ready, i - 1)
                    transposes(bank, lambda b: xin[:, 1 - p, b, :], xt_done)
                if t == 2 and s.prev:
                    if isinstance(i, int) and i == 1:
                        pe.wait_ge(gates_in, 32)
                    pe.wait_ge(acc_ready, i * 3)
                    after(pe, kt_ready, i - 2 + 1)
                    for n, a in enumerate((2, 0, 1)):
                        tok0 = acc_sb[:, 1 - p, a].rearrange("d (b n) -> d b n", b=GB)[:, :, 0]
                        mm = pe.matmul(bank[:, 0:GB], g1_sb[:, n, :], tok0, start=(n == 0), stop=(n == 2))
                    mm.then_inc(g1_done, 1)
                if t == 3 and s.attn:
                    pe.wait_ge(xq_ready, i - 1 + HEAD)
                    after(pe, xt_ready, i + 2) if s.prep else None
                    transposes(bank, lambda b: cols(xq, b), x3t_done)
                if t == 4 and s.prev:
                    pe.wait_ge(gprod_ready, i)
                    mm = pe.matmul(bank[:, 0:GB * 3], ones[:, :], gprod[:, :, :].rearrange("j b k -> j (b k)"),
                                   start=True, stop=True)
                    mm.then_inc(g2_done, 1)
                if t == 5 and s.attn:
                    pe.wait_ge(qt_ready, i - 1)
                    pe.wait_ge(kt_ready, i - 1)
                    for b in range(GB):
                        mm = pe.matmul(cols(bank, b), cols(qT, b), cols(kT, b), start=True, stop=True)
                    mm.then_inc(qk_done, 1)
                if t == 6 and s.prep:
                    pe.wait_ge(xt_ready, i + 2)
                    pe.wait_ge(w0_sel_in, (i + 2) * (16 * GB))
                    if s.prev:
                        pe.wait_ge(gsub_ready, i)
                    for b in range(GB):
                        mm = pe.matmul(cols(bank, b), w0_sel[:, b, :], cols(xT, b), start=True, stop=True)
                    mm.then_inc(l0_done, 1)
                if t == 7 and s.attn:
                    pe.wait_ge(probs_ready, i - 1)
                    transposes(bank, lambda b: cols(probs, b), pt_done)
                if t == 8 and s.prev:
                    pe.wait_ge(mixed, i * 3)
                    if s.prep:
                        pe.wait_ge(x1_ready, i + 2)
                    transposes(bank, lambda b: cols(x2T, b), x2n_done)
                if t == 9 and s.prev:
                    pe.wait_ge(l2w_in, i * (32 * GB))
                    if s.attn:
                        pe.wait_ge(pt_ready, i - 1)
                    for b in range(GB):
                        mm = pe.matmul(cols(bank, b), wd_sel[:, b, :], cols(x2T, b), start=True, stop=True)
                    mm.then_inc(z_done, 1)
                if t == 10 and s.attn:
                    pe.wait_ge(pt_ready, i - 1)
                    if s.prev:
                        pe.wait_ge(x2n_ready, i)
                    for b in range(GB):
                        mm = pe.matmul(cols(bank, b), cols(pT, b), keys[:, p, b, :], start=True, stop=True)
                    mm.then_inc(pv_done, 1)
                if t == 11 and s.prev:
                    pe.wait_ge(zt_ready, i)
                    for b in range(GB):
                        mm = pe.matmul(cols(bank, b), cols(zT, b), wu_sel[:, b, :], start=True, stop=True)
                    mm.then_inc(y_done, 1)

            def slot(s):
                for t in range(UNITS):
                    if s.mlp:
                        hidden(t, s)
                    if t >= 2 and s.mlp:
                        output(t - 2, s.i)
                    if t < 2 and s.prev:
                        output(t + UNITS - 2, s.i - 1)
                    piece(t, s)

            run_slots(pe, slot)

        @block.scalar
        def _(act):
            for half_ in range(2):
                act.wait_ge(w0t_done, half_ + 1)
                act.activation(w0_table[:, half_ * GB:(half_ + 1) * GB, :].rearrange("p s o -> p (s o)"),
                               misc[half_][:, :], ACT.Copy).then_inc(w0tab_ready, 1)

            def table_hi(n):
                act.wait_ge(stage_in[n % 2], 32 * (n // 2 + 1))
                act.activation(TABLES[n][0][:, 0], stage[:, n % 2], ACT.Copy).then_inc(tab_hi, 1)

            def setup(i):
                if i == -1:
                    table_hi(0)
                    table_hi(1)
                if i == 0:
                    for n in range(2, 2 + E):
                        table_hi(n)

            def slot(s):
                i, p = s.i, s.p

                def relu_hi(k):
                    act.wait_ge(hid_done, i * UNITS + k + 1)
                    after(act, out_done, i * UNITS + k - 3)
                    act.activation(hid_hi[:, k % 4], hid_ps[k % 3][:, :], ACT.Relu).then_inc(hi_ready, 1)

                def acc_out(a, g, q):
                    act.wait_ge(out_done, g * UNITS + (FC, 2 * FC, UNITS)[a])
                    if a == 0:
                        after(act, mixed, g * 3 - 3)
                    act.activation(acc_sb[:, q, a], acc_ps[a][:, :], ACT.Copy).then_inc(acc_ready, 1)

                for t in range(UNITS):
                    if s.mlp:
                        relu_hi(t)
                    if t == 0 and s.attn:
                        act.wait_ge(kt_done, i - 1)
                        after(act, qk_done, i - 2 + HEAD)
                        act.activation(kT[:, :], misc[0][:, :], ACT.Copy).then_inc(kt_ready, 1)
                    if t == 1 and s.prev:
                        acc_out(2, i - 1, 1 - p)
                    if t == 1 and s.prep:
                        act.wait_ge(xt_done, i + 2)
                        after(act, x1_ready, i + 1)
                        act.activation(xT[:, :], misc[1][:, :], ACT.Copy).then_inc(xt_ready, 1)
                    if t == 3 and s.attn:
                        act.wait_ge(x3t_done, i - 1 + HEAD)
                        act.activation(qT[:, :], misc[1][:, :], ACT.Copy).then_inc(qt_ready, 1)
                    if t == 5 and s.prev:
                        act.wait_ge(gsub_ready, i)
                        act.activation(gexp[:, :, :], gsub[:, :, :], ACT.Exp).then_inc(gexp_ready, 1)
                    if t == 5 and s.mlp:
                        acc_out(0, i, p)
                    if t == 6 and s.attn:
                        act.wait_ge(negmax_ready, i - 1)
                        after(act, prec_ready, i - 2 + HEAD)
                        for b in range(GB):
                            op = act.activation(cols(probs, b), cols(misc[1], b), ACT.Exp, bias=negmax[:, b:b + 1],
                                                accum_out=psums[:, b:b + 1])
                        op.then_inc(probs_ready, 1)
                    if t == 7 and s.prep:
                        act.wait_ge(x1_ready, i + 2)
                        act.activation(x1h[:, 1 - p], x1T[:, 1 - p], ACT.Copy).then_inc(x1h_ready, 1)
                    if t == 7 and s.attn:
                        act.wait_ge(pt_done, i - 1)
                        act.activation(pT[:, :], misc[1][:, :], ACT.Copy).then_inc(pt_ready, 1)
                    if t == 8 and s.prev:
                        act.wait_ge(x2n_done, i)
                        after(act, x3_ready, i - 1 + HEAD)
                        act.activation(x2n[:, :], misc[0][:, :], ACT.Copy).then_inc(x2n_ready, 1)
                    if t == 9 and s.mlp:
                        acc_out(1, i, p)
                    if t == 9 and s.prev:
                        act.wait_ge(z_done, i)
                        act.wait_ge(bd_sel_ready, i)
                        after(act, y_done, i - 1)
                        for b in range(GB):
                            op = act.activation(cols(zT, b), cols(misc[1], b), ACT.Relu, bias=bd_sel[:, b:b + 1])
                        op.then_inc(zt_ready, 1)

            run_slots(act, slot, setup)

        @block.vector
        def _(dve):
            for s_ in (o_ready, prec_ready,):
                dve.sem_inc(s_, HEAD)
            dve.wait_ge(consts, 4)
            dve.tensor_copy(row_f[:, :], row_i[:, :]).then_inc(rowf_ready, 1)
            dve.wait_ge(rowf_ready, 1)
            dve.wait_ge(idrows_in, 96)
            for n, rows in enumerate((P0, P2, P3)):
                op = dve.tensor_scalar(onehot[0:rows, n, :], ids_rows[0:rows, n, :], row_f[0:rows, :], None, ALU.is_equal)
            op.then_inc(onehot_ready, 1)
            dve.wait_ge(cols_done, 1)
            dve.tensor_copy(columns[:, :, :].rearrange("p n b -> p (n b)"), hid_ps[0][:, 0:3 * B]).then_inc(cols_ready, 1)

            def table_lo(n):
                dve.wait_ge(tab_hi, n + 1)
                dve.tensor_tensor(TABLES[n][0][:, 1], stage[:, n % 2], TABLES[n][0][:, 0].bitcast(F32),
                                  ALU.subtract).then_inc(tab_lo, 1)

            def setup(i):
                if i == -1:
                    table_lo(0)
                    table_lo(1)
                if i == 0:
                    for n in range(2, 2 + E):
                        table_lo(n)

            def per_batch(a):
                return a.unsqueeze(2).broadcast_to([128, GB, 3])

            def ln_rstd(g):
                n = [0]

                def chained(op):
                    op.then_inc(ln_steps, 1)
                    n[0] += 1
                    dve.wait_ge(ln_steps, g * LN_STEPS + n[0])

                dve.wait_ge(meanvar_ready, g + 1)
                chained(dve.tensor_scalar(var[:, :], meanvar[:, :, 1], EPS, None, ALU.add))
                chained(dve.tensor_scalar(half[:, :], var[:, :].bitcast(I32), 1, None, ALU.arith_shift_right))
                chained(dve.tensor_scalar(rstd[:, :].bitcast(I32), half[:, :], -1.0, RSQRT_MAGIC, ALU.mult, ALU.add))
                for _ in range(NEWTON):
                    chained(dve.tensor_tensor(nt[:, 0], rstd[:, :], rstd[:, :], ALU.mult))
                    chained(dve.scalar_tensor_tensor(out=nt[:, 1], in0=nt[:, 0], scalar=-0.5, in1=var[:, :],
                                                     op0=ALU.mult, op1=ALU.mult))
                    chained(dve.scalar_tensor_tensor(out=rstd[:, :], in0=nt[:, 1], scalar=1.5, in1=rstd[:, :],
                                                     op0=ALU.add, op1=ALU.mult))

            def slot(s):
                i, p = s.i, s.p

                def relu_lo(k):
                    dve.wait_ge(hi_ready, i * UNITS + k + 1)
                    dve.scalar_tensor_tensor(out=hid_lo[:, k % 4], in0=hid_ps[k % 3][:, :], scalar=0.0,
                                             in1=hid_hi[:, k % 4].bitcast(F32), op0=ALU.max, op1=ALU.subtract).then_inc(lo_ready, 1)

                def mix(n):
                    src = x1T[:, 1 - p] if n == 0 else x2T[:, :]
                    for b in range(GB):
                        op = dve.scalar_tensor_tensor(out=cols(x2T, b), in0=cols(acc_sb[:, 1 - p, (2, 0, 1)[n]], b),
                                                      scalar=gate[:, b, n:n + 1], in1=cols(src, b), op0=ALU.mult, op1=ALU.add)
                    op.then_inc(mixed, 1)

                if s.attn:
                    dve.wait_ge(stats_ready, i - 1)
                for t in range(UNITS):
                    if s.mlp:
                        relu_lo(t)
                    if t == 0 and s.attn:
                        for b in range(GB):
                            op = dve.bn_aggr(meanvar[:, b, :], stats[:, b, :])
                        op.then_inc(meanvar_ready, 1)
                        ln_rstd(i - 2)
                    if t == 1 and s.attn:
                        after(dve, x3_ready, i - 2 + HEAD)
                        for b in range(GB):
                            op = dve.tensor_scalar(cols(yn, b), cols(y, b), meanvar[:, b, 0:1], rstd[:, b:b + 1],
                                                   ALU.subtract, ALU.mult)
                        op.then_inc(yn_ready, 1)
                    if t == 2 and s.prev:
                        dve.wait_ge(g1_done, i)
                        after(dve, g2_done, i - 1)
                        dve.scalar_tensor_tensor(out=gprod[:, :, :], in0=per_batch(misc[0][:, 0:GB]), scalar=0.0,
                                                 in1=g2_sb[:, :].unsqueeze(1).broadcast_to([128, GB, 3]),
                                                 op0=ALU.max, op1=ALU.mult).then_inc(gprod_ready, 1)
                    if t == 4 and s.prev:
                        dve.wait_ge(g2_done, i)
                        logits = misc[0][:, 0:GB * 3].rearrange("p (b k) -> p b k", b=GB)
                        dve.tensor_reduce(gmax[:, :], logits, AX.X, ALU.max).then_inc(gmax_ready, 1)
                        dve.wait_ge(gmax_ready, i)
                        dve.tensor_tensor(gsub[:, :, :], logits, per_batch(gmax[:, :]), ALU.subtract).then_inc(gsub_ready, 1)
                    if t == 5 and s.attn:
                        dve.wait_ge(qk_done, i - 1 + HEAD)
                        dve.tensor_reduce(negmax[:, :], misc[1][:, :].rearrange("p (b n) -> p b n", b=GB), AX.X, ALU.max,
                                          negate=True).then_inc(negmax_ready, 1)
                    if t == 5 and s.prev:
                        dve.wait_ge(gexp_ready, i)
                        dve.tensor_reduce(gsum[:, :], gexp[:, :, :], AX.X, ALU.add).then_inc(gate_steps, 1)
                        dve.wait_ge(gate_steps, i * 3 - 2)
                        dve.reciprocal(grec[:, :], gsum[:, :]).then_inc(gate_steps, 1)
                        dve.wait_ge(gate_steps, i * 3 - 1)
                        dve.tensor_tensor(gate[:, :, :], gexp[:, :, :], per_batch(grec[:, :]), ALU.mult).then_inc(gate_steps, 1)
                        dve.wait_ge(gate_steps, i * 3)
                        dve.wait_ge(acc_ready, i * 3)
                        after(dve, z_done, i - 1)
                        mix(0)
                    if t == 6 and s.prep:
                        if s.prev:
                            dve.wait_ge(mixed, i * 3 - 2)
                        dve.wait_ge(l0_done, i + 2)
                        dve.wait_ge(b0_sel_ready, i + 2)
                        for b in range(GB):
                            op = dve.scalar_tensor_tensor(out=cols(x1T[:, 1 - p], b), in0=cols(misc[0], b),
                                                          scalar=b0_sel[:, b:b + 1], in1=cols(xT, b), op0=ALU.add, op1=ALU.add)
                        op.then_inc(x1_ready, 1)
                    if t == 6 and s.prev:
                        dve.wait_ge(mixed, i * 3 - 2)
                        mix(1)
                    if t == 7 and s.prev:
                        dve.wait_ge(mixed, i * 3 - 1)
                        mix(2)
                    if t == 7 and s.attn:
                        dve.wait_ge(probs_ready, i - 1)
                        dve.reciprocal(prec[:, :], psums[:, :]).then_inc(prec_ready, 1)
                    if t == 10 and s.attn:
                        dve.wait_ge(pv_done, i - 1 + HEAD)
                        dve.wait_ge(prec_ready, i - 1 + HEAD)
                        after(dve, stored, i * 16 - 32 + 16 * HEAD)
                        for b in range(GB):
                            op = dve.scalar_tensor_tensor(out=cols(o_sb, b), in0=cols(misc[0], b), scalar=prec[:, b:b + 1],
                                                          in1=cols(x3, b), op0=ALU.mult, op1=ALU.add)
                        op.then_inc(o_ready, 1)
                    if t == 11 and s.prev:
                        dve.wait_ge(y_done, i)
                        dve.wait_ge(x2b_ready, i)
                        after(dve, yn_ready, i - 1)
                        dve.tensor_tensor(y[:, :], misc[1][:, :], x2b[:, :], ALU.add).then_inc(y_ready, 1)
                        dve.wait_ge(y_ready, i)
                        after(dve, meanvar_ready, i - 1)
                        for b in range(GB):
                            op = dve.bn_stats(stats[:, b, :], cols(y, b))
                        op.then_inc(stats_ready, 1)

            run_slots(dve, slot, setup)

        @block.gpsimd
        def _(pool):
            for s_ in (x3_ready, xq_ready,):
                pool.sem_inc(s_, HEAD)
            pool.memset(ones[:, :], 1.0).then_inc(consts, 1)
            pool.memset(ident[:, :], 0.0).then_inc(consts, 1)
            pool.wait_ge(consts, 2)
            pool.affine_select(out=ident[:, :], in_=ident[:, :], compare_op=ALU.not_equal, fill=1.0,
                               base=0, pattern=[[-1, 128]], channel_multiplier=1).then_inc(consts, 1)
            pool.iota(row_i[:, :], [[0, 1]], base=0, channel_multiplier=1).then_inc(consts, 1)
            pool.wait_ge(cols_ready, 1)
            pool.wait_ge(ids_in, 64)
            pool.wait_ge(lntab_in, 48)

            def ln_row(n, g, b):
                who = pool.value_load(ids[0:1, 2, bass.ds(g * GB + b, 1)], min_val=0, max_val=P2 - 1)
                return [ln_table[:, m, bass.ds(who, 1), :].rearrange("p s d -> p (s d)") for m in n]

            def slot(s):
                i, p = s.i, s.p
                if s.attn:
                    after(pool, xq_ready, i - 2 + HEAD)
                    pool.tensor_copy(em_sel[:, :], columns[:, 2, bass.ds(i * GB - 2 * GB, GB)]).then_inc(em_sel_ready, 1)
                if s.prep:
                    after(pool, x1_ready, i + 1)
                    pool.tensor_copy(b0_sel[:, :], columns[:, 0, bass.ds((i * GB + GB) % B, GB)]).then_inc(b0_sel_ready, 1)
                if s.prev:
                    after(pool, zt_ready, i - 1)
                    pool.tensor_copy(bd_sel[:, :], columns[:, 1, bass.ds(i * GB - GB, GB)]).then_inc(bd_sel_ready, 1)
                if s.attn:
                    rows = [ln_row((1, 2), i - 2, b) for b in range(GB)]
                    pool.wait_ge(yn_ready, i - 1)
                    after(pool, o_ready, i - 2 + HEAD)
                    for b in range(GB):
                        op = pool.tensor_tensor(cols(yg, b), cols(yn, b), rows[b][0], ALU.mult)
                    op.then_inc(yg_steps, 1)
                    pool.wait_ge(yg_steps, i * 2 - 3)
                    for b in range(GB):
                        op = pool.tensor_tensor(cols(yg, b), cols(yg, b), rows[b][1], ALU.add)
                    op.then_inc(yg_steps, 1)
                    pool.wait_ge(yg_steps, i * 2 - 2)
                    pool.tensor_tensor(x3[:, :], yg[:, :], x2n[:, :], ALU.add).then_inc(x3_ready, 1)
                    pool.wait_ge(x3_ready, i - 1 + HEAD)
                    pool.wait_ge(em_sel_ready, i - 1)
                    after(pool, x3t_done, i - 2 + HEAD)
                    pool.tensor_tensor(xq[:, :].rearrange("n (b d) -> n b d", b=GB), x3[:, :].rearrange("n (b d) -> n b d", b=GB),
                                       em_sel[:, :].unsqueeze(2).broadcast_to([128, GB, 128]), ALU.add).then_inc(xq_ready, 1)
                if s.prep:
                    pool.wait_ge(x1h_ready, i + 2)
                    pool.tensor_tensor(x1l[:, 1 - p], x1T[:, 1 - p], x1h[:, 1 - p].bitcast(F32),
                                       ALU.subtract).then_inc(x1l_ready, 1)
                if s.prev:
                    rows = [ln_row((0,), i - 1, b) for b in range(GB)]
                    pool.wait_ge(x2n_ready, i)
                    after(pool, y_ready, i - 1)
                    for b in range(GB):
                        op = pool.tensor_tensor(cols(x2b, b), cols(x2n, b), rows[b][0], ALU.add)
                    op.then_inc(x2b_ready, 1)

            run_slots(pool, slot)


_INS = ["x", "itok_B_0_7", "itok_B_0_2", "itok_B_0_6", "fside_BxSxS_0", "itok_B_0_5",
        "L0_cond_weight", "L0_cond_bias", "L1_cond_wi", "L1_cond_wo", "L1_cond_swi", "L1_cond_swo",
        "L1_cond_g1", "L1_cond_g2", "L2_cond_down_w", "L2_cond_down_b", "L2_cond_up_w", "L2_cond_up_b",
        "L2_cond_ln_g", "L2_cond_ln_b", "L3_cond_braak_embed"]


def kernel(**inputs):
    import numpy as _np
    import concourse.bacc as _bacc
    from concourse import mybir as _mybir
    from concourse.bass_utils import run_bass_kernel_spmd as _run

    nc = _bacc.Bacc("TRN2", target_bir_lowering=False, num_devices=1)
    arrays, args = {}, []
    for name in _INS:
        a = _np.ascontiguousarray(inputs[name])
        arrays[f"in_{name}_dram"] = a
        args.append(nc.dram_tensor(f"in_{name}_dram", a.shape, _mybir.dt.from_np(a.dtype), kind="ExternalInput").ap())
    shape = inputs["x"].shape
    args.append(nc.dram_tensor("out_0_dram", shape, _mybir.dt.float32, kind="ExternalOutput").ap())
    build(nc, *args)
    r = _run(nc, [arrays], core_ids=[0])
    return r.results[0]["out_0_dram"]
```

```python
from contextlib import ExitStack

import concourse.bass as bass
from concourse import mybir

F32 = mybir.dt.float32
F32R = mybir.dt.float32r
I32 = mybir.dt.int32
ALU = mybir.AluOpType
ACT = mybir.ActivationFunctionType
AX = mybir.AxisListType

GB = 4
UNITS = 12
NSH = 8
EPS = 1e-5
RSQRT_MAGIC = float(0x5F3759DF)
NEWTON = 3
HEAD = 1
LN_STEPS = 3 + 3 * NEWTON
WRAP_FIRST, WRAP_LAST = 2, 7


def after(eng, sem, count):
    if isinstance(count, int) and count <= 0:
        return
    eng.wait_ge(sem, count)


class Slot:

    def __init__(self, i, p, h, prep, mlp, prev, attn):
        self.i, self.p, self.h = i, p, h
        self.prep = prep
        self.mlp = mlp
        self.prev = prev
        self.attn = attn


def run_slots(eng, body, before_slot=None):
    for i, flags in ((-1, (1, 0, 0, 0)), (0, (1, 1, 0, 0)), (1, (1, 1, 1, 0))):
        if before_slot:
            before_slot(i)
        body(Slot(i, i % 2, i // 2, *flags))
    with eng.Fori(WRAP_FIRST // 2, (WRAP_LAST + 1) // 2) as pair:
        for p in range(2):
            body(Slot(pair * 2 + p, p, pair, 1, 1, 1, 1))
    body(Slot(8, 0, 4, 0, 0, 1, 1))
    body(Slot(9, 1, 4, 0, 0, 0, 1))


def build(nc, x, id7, id2, id6, side, id5, w0, b0, wi, wo, swi, swo, g1, g2,
          down_w, down_b, up_w, up_b, ln_g, ln_b, embed, out):
    B, N, D = x.shape
    E, _, F = wi.shape
    P0, P2, P3 = w0.shape[0], down_w.shape[0], embed.shape[0]
    FC = F // D
    W = GB * N
    NG = B // GB
    RAW = F + FC * D
    assert N == D == 128 and W == 512 and FC == 4 and NG == 8

    with ExitStack() as ctx:
        def sb(name, shape, dt=F32):
            return ctx.enter_context(nc.sbuf_tensor(name, shape, dt))

        def sem(name):
            return ctx.enter_context(nc.semaphore(name))

        shared = sb("shared", [128, 2, 2, RAW], F32R)
        w0_table = sb("w0_table", [128, P0, 128])
        ln_table = sb("ln_table", [128, 3, P2, 128])
        em_table = sb("em_table", [128, P3, 128])
        columns = sb("columns", [128, 2, B])
        g1_sb = sb("g1_sb", [128, 3, 128])
        g2_sb = sb("g2_sb", [128, 3])
        ident = sb("ident", [128, 128])
        ones = sb("ones", [128, 128])
        ids = sb("ids", [1, 4, B], I32)
        stage = sb("stage", [128, 2, RAW])
        w0_raw = sb("w0_raw", [128, P0, 128])
        ids_rows = sb("ids_rows", [P0, 2, B], I32)
        row_i = sb("row_i", [P0, 1], I32)
        row_f = sb("row_f", [P0, 1])
        onehot = sb("onehot", [P0, 2, B])
        bias_rows = sb("bias_rows", [P0, 2, 128])
        esel = sb("esel", [128, GB, RAW])
        w0_sel = sb("w0_sel", [128, GB, 128])
        wd_sel = sb("wd_sel", [128, GB, 128])
        wu_sel = sb("wu_sel", [128, GB, 128])
        b0_sel = sb("b0_sel", [128, GB])
        bd_sel = sb("bd_sel", [128, GB])
        g_sel = sb("g_sel", [128, GB, 128])
        em_sel = sb("em_sel", [128, GB, 128])
        xin = sb("xin", [128, 2, GB, 128])
        keys = sb("keys", [128, 2, GB, 128])
        xT = sb("xT", [128, W])
        x1T = sb("x1T", [128, 2, W])
        x1h = sb("x1h", [128, 2, W], F32R)
        x1l = sb("x1l", [128, 2, W], F32R)
        hid_hi = sb("hid_hi", [128, 4, W], F32R)
        hid_lo = sb("hid_lo", [128, 4, W], F32R)
        hid_f = sb("hid_f", [128, GB, W])
        acc_sb = sb("acc_sb", [128, 2, 3, W])
        gprod = sb("gprod", [128, GB, 3])
        gmax = sb("gmax", [128, GB])
        gsub = sb("gsub", [128, GB, 3])
        gexp = sb("gexp", [128, GB, 3])
        gsum = sb("gsum", [128, GB])
        grec = sb("grec", [128, GB])
        gate = sb("gate", [128, GB, 3])
        x2T = sb("x2T", [128, W])
        x2n = sb("x2n", [128, W])
        x2b = sb("x2b", [128, W])
        zT = sb("zT", [128, W])
        y = sb("y", [128, W])
        stats = sb("stats", [128, GB, 6])
        meanvar = sb("meanvar", [128, GB, 2])
        var = sb("var", [128, GB])
        half = sb("half", [128, GB], I32)
        rstd = sb("rstd", [128, GB])
        nt = sb("nt", [128, 2, GB])
        yg = sb("yg", [128, W])
        x2nb = sb("x2nb", [128, W])
        x3 = sb("x3", [128, W])
        qT = sb("qT", [128, W])
        kT = sb("kT", [128, W])
        negmax = sb("negmax", [128, GB])
        probs = sb("probs", [128, W])
        psums = sb("psums", [128, GB])
        prec = sb("prec", [128, GB])
        pT = sb("pT", [128, W])
        o_sb = sb("o_sb", [128, W])

        hid_ps = [ctx.enter_context(nc.psum_tensor(f"hid_ps{n}", [128, W], F32)) for n in range(3)]
        acc_ps = [ctx.enter_context(nc.psum_tensor(f"acc_ps{n}", [128, W], F32)) for n in range(3)]
        misc = [ctx.enter_context(nc.psum_tensor(f"misc{n}", [128, W], F32)) for n in range(2)]

        ids_in = sem("ids_in")
        idrows_in = sem("idrows_in")
        w0_in = sem("w0_in")
        gates_in = sem("gates_in")
        lntab_in = sem("lntab_in")
        stage_in = [sem("stage_in0"), sem("stage_in1")]
        consts = sem("consts")
        w0t_done = sem("w0t_done")
        w0tab_ready = sem("w0tab_ready")
        rowf_ready = sem("rowf_ready")
        onehot_ready = sem("onehot_ready")
        cols_done = sem("cols_done")
        cols_ready = sem("cols_ready")
        tab_hi = sem("tab_hi")
        tab_lo = sem("tab_lo")
        x_in = [sem("x_in0"), sem("x_in1")]
        k_in = [sem("k_in0"), sem("k_in1")]
        w0_sel_in = sem("w0_sel_in")
        l2w_in = sem("l2w_in")
        esel_in = [sem(f"esel_in{b}") for b in range(GB)]
        stored = sem("stored")
        hid_done = sem("hid_done")
        out_done = sem("out_done")
        kt_done, xt_done, g1_done, x3t_done = sem("kt_done"), sem("xt_done"), sem("g1_done"), sem("x3t_done")
        g2_done, qk_done, l0_done, pt_done = sem("g2_done"), sem("qk_done"), sem("l0_done"), sem("pt_done")
        x2n_done, z_done, pv_done, y_done = sem("x2n_done"), sem("z_done"), sem("pv_done"), sem("y_done")
        hi_ready = sem("hi_ready")
        acc_ready = sem("acc_ready")
        kt_ready, xt_ready = sem("kt_ready"), sem("xt_ready")
        gexp_ready, probs_ready, x1h_ready = sem("gexp_ready"), sem("probs_ready"), sem("x1h_ready")
        pt_ready, x2n_ready, zt_ready = sem("pt_ready"), sem("x2n_ready"), sem("zt_ready")
        lo_ready = sem("lo_ready")
        gprod_ready, gmax_ready, gsub_ready = sem("gprod_ready"), sem("gmax_ready"), sem("gsub_ready")
        gate_steps, mixed = sem("gate_steps"), sem("mixed")
        negmax_ready, x1_ready, prec_ready = sem("negmax_ready"), sem("x1_ready"), sem("prec_ready")
        o_ready, y_ready = sem("o_ready"), sem("y_ready")
        stats_ready, meanvar_ready = sem("stats_ready"), sem("meanvar_ready")
        ln_steps, yg_ready = sem("ln_steps"), sem("yg_ready")
        x3_ready, qt_ready = sem("x3_ready"), sem("qt_ready")
        b0_sel_ready, bd_sel_ready = sem("b0_sel_ready"), sem("bd_sel_ready")
        x2nb_ready, g_sel_ready, em_sel_ready = sem("x2nb_ready"), sem("g_sel_ready"), sem("em_sel_ready")
        x1l_ready, x2b_ready = sem("x1l_ready"), sem("x2b_ready")

        block = ctx.enter_context(nc.Block())

        def cols(t, b):
            return t[:, b * 128:(b + 1) * 128]


        @block.sync
        def _(sp):
            sp.sem_inc(stored, 16 * HEAD)
            for n, t in enumerate((id7, id2, id6, id5)):
                sp.dma_start(ids[0:1, n, :], t.rearrange("(a b) -> a b", a=1)).then_inc(ids_in, 16)
            sp.dma_start(w0_raw[:, :, :], w0.rearrange("s o h -> o s h")).then_inc(w0_in, 16)

            def load_x(g, p):
                first = (g * GB) % B
                sp.dma_start(xin[:, p], x[bass.ds(first, GB)].rearrange("b n d -> n b d")).then_inc(x_in[p], 16)

            def load_w0(g):
                for b in range(GB):
                    who = sp.value_load(ids[0:1, 0, bass.ds((g * GB + b) % B, 1)], min_val=0, max_val=P0 - 1)
                    sp.dma_start(w0_sel[:, b, :], w0_table[:, bass.ds(who, 1), :]).then_inc(w0_sel_in, 16)

            def load_stage(e):
                sp.dma_start(stage[:, e, 0:F], swi[e]).then_inc(stage_in[e], 16)
                sp.dma_start(stage[:, e, F:RAW].rearrange("p (c d) -> p c d", c=FC),
                             swo[e].rearrange("(c p) d -> p c d", p=128)).then_inc(stage_in[e], 16)

            load_x(0, 0)
            for n, (t, rows) in enumerate(((id7, P0), (id6, P2))):
                sp.dma_start(ids_rows[0:rows, n, :], t.partition_broadcast(rows)).then_inc(idrows_in, 16)
            for n, (t, rows) in enumerate(((b0, P0), (down_b, P2))):
                sp.dma_start(bias_rows[0:rows, n, :], t).then_inc(idrows_in, 16)
            load_stage(0)
            load_stage(1)
            sp.wait_ge(ids_in, 64)
            sp.wait_ge(w0tab_ready, 2)
            load_w0(0)
            for n, t in enumerate((up_b, ln_g, ln_b)):
                sp.dma_start(ln_table[:, n], t.partition_broadcast(128)).then_inc(lntab_in, 16)
            sp.dma_start(g1_sb[:, :, :], g1.rearrange("(c p) j -> p c j", p=128)).then_inc(gates_in, 16)
            sp.dma_start(g2_sb[:, :], g2).then_inc(gates_in, 16)
            sp.dma_start(em_table[:, :, :], embed.partition_broadcast(128)).then_inc(lntab_in, 16)

            def slot(s):
                i, p, h = s.i, s.p, s.h
                if s.prev:
                    after(sp, y_done, i - 1)
                    for b in range(GB):
                        who = sp.value_load(ids[0:1, 2, bass.ds(i * GB - GB + b, 1)], min_val=0, max_val=P2 - 1)
                        sp.dma_start(wd_sel[:, b, :], down_w[bass.ds(who, 1)].rearrange("s h k -> (s h) k")).then_inc(l2w_in, 16)
                        sp.dma_start(wu_sel[:, b, :], up_w[bass.ds(who, 1)].rearrange("s k h -> (s k) h")).then_inc(l2w_in, 16)
                if s.mlp:
                    for b in range(GB):
                        after(sp, out_done, i * UNITS - GB + b + 1)
                        who = sp.value_load(ids[0:1, 1, bass.ds(i * GB + b, 1)], min_val=0, max_val=E - 1)
                        sp.dma_start(esel[:, b, 0:F], wi[bass.ds(who, 1)].rearrange("e d f -> (e d) f")).then_inc(esel_in[b], 16)
                        sp.dma_start(esel[:, b, F:RAW].rearrange("p (c d) -> p c d", c=FC),
                                     wo[bass.ds(who, 1)].rearrange("e (c p) d -> p (e c) d", p=128)).then_inc(esel_in[b], 16)
                if s.prev:
                    after(sp, pv_done, i - 2 + HEAD)
                    sp.dma_start(keys[:, 1 - p], side[bass.ds(i * GB - GB, GB)].rearrange("b n d -> n b d")).then_inc(k_in[1 - p], 16)
                if s.prep:
                    after(sp, xt_done, i + 1)
                    load_x(i + 2, p)
                    after(sp, l0_done, i + 2)
                    load_w0(i + 2)
                if s.attn:
                    after(sp, o_ready, i - 1 + HEAD)
                    sp.dma_start(out[bass.ds(i * GB - 2 * GB, GB)].rearrange("b n d -> n b d"),
                                 o_sb[:, :].rearrange("n (b d) -> n b d", b=GB)).then_inc(stored, 16)

            run_slots(sp, slot)
            sp.wait_ge(x_in[0], 16 * (NG // 2 + 1))
            sp.wait_ge(x_in[1], 16 * (NG // 2 + 1))
            sp.wait_ge(w0_sel_in, 16 * GB * (NG + 2))
            sp.wait_ge(stored, 16 * (NG + HEAD))

        @block.tensor
        def _(pe):
            for s_ in (qk_done, x3t_done, pv_done,):
                pe.sem_inc(s_, HEAD)
            def transposes(bank, src, done):
                for b in range(GB):
                    mm = pe.transpose(cols(bank, b), src(b), ident[:, :])
                mm.then_inc(done, 1)

            pe.wait_ge(consts, 3)
            pe.wait_ge(w0_in, 16)
            for half_ in range(2):
                transposes(misc[half_], lambda b: w0_raw[:, half_ * GB + b, :], w0t_done)
            pe.wait_ge(idrows_in, 64)
            pe.wait_ge(onehot_ready, 1)
            for n, rows in enumerate((P0, P2)):
                mm = pe.matmul(hid_ps[0][:, n * B:(n + 1) * B], bias_rows[0:rows, n, :], onehot[0:rows, n, :],
                               start=True, stop=True)
            mm.then_inc(cols_done, 1)
            pe.wait_ge(w0tab_ready, 2)

            def hidden(k, s):
                i, p = s.i, s.p
                bank = hid_ps[k % 3]
                if k == 0:
                    pe.wait_ge(x1h_ready, i + 1)
                    pe.wait_ge(x1l_ready, i + 1)
                    if isinstance(i, int) and i == 0:
                        pe.wait_ge(cols_ready, 1)
                if k < 3:
                    after(pe, hi_ready, i * UNITS + k - 2)
                elif k - 3 < NSH:
                    pe.wait_ge(lo_ready, i * NSH + k - 2)
                if k < NSH:
                    e, c = k // FC, k % FC
                    if isinstance(i, int) and i == 0 and c == 0:
                        pe.wait_ge(tab_lo, e + 1)
                    w_hi, w_lo = cols(shared[:, e, 0], c), cols(shared[:, e, 1], c)
                    pe.matmul(bank[:, :], w_hi, x1h[:, p], start=True, stop=False)
                    pe.matmul(bank[:, :], w_lo, x1h[:, p], start=False, stop=False)
                    mm = pe.matmul(bank[:, :], w_hi, x1l[:, p], start=False, stop=True)
                else:
                    b = k - NSH
                    pe.wait_ge(esel_in[b], i * 32 + 32)
                    for c in range(FC):
                        mm = pe.matmul(cols(bank, c), cols(esel[:, b], c), cols(x1T[:, p], b), start=True, stop=True)
                mm.then_inc(hid_done, 1)

            def output(k, i):
                if k < NSH:
                    pe.wait_ge(lo_ready, i * NSH + k + 1)
                    h_hi, h_lo = hid_hi[:, k % 4], hid_lo[:, k % 4]
                    e, c = k // FC, k % FC
                    if c == 0:
                        after(pe, acc_ready, i * 3 - 2 + e)
                    w_hi, w_lo = cols(shared[:, e, 0], FC + c), cols(shared[:, e, 1], FC + c)
                    pe.matmul(acc_ps[e][:, :], w_hi, h_hi, start=(c == 0), stop=False)
                    pe.matmul(acc_ps[e][:, :], w_lo, h_hi, start=False, stop=False)
                    mm = pe.matmul(acc_ps[e][:, :], w_hi, h_lo, start=False, stop=(c == FC - 1))
                else:
                    b = k - NSH
                    pe.wait_ge(hi_ready, i * UNITS + k + 1)
                    if b == 0:
                        after(pe, acc_ready, i * 3)
                    for c in range(FC):
                        mm = pe.matmul(cols(acc_ps[2], b), cols(esel[:, b], FC + c), cols(hid_f[:, b], c),
                                       start=(c == 0), stop=(c == FC - 1))
                mm.then_inc(out_done, 1)

            def piece(t, s):
                i, p, h = s.i, s.p, s.h
                bank = misc[t % 2]
                if t == 0 and s.attn:
                    pe.wait_ge(k_in[p], h * 16)
                    after(pe, y_ready, i - 1)
                    transposes(bank, lambda b: keys[:, p, b, :], kt_done)
                if t == 1 and s.prep:
                    pe.wait_ge(x_in[1 - p], (h + 1 + p) * 16)
                    after(pe, o_ready, i - 2 + HEAD)
                    transposes(bank, lambda b: xin[:, 1 - p, b, :], xt_done)
                if t == 2 and s.prev:
                    if isinstance(i, int) and i == 1:
                        pe.wait_ge(gates_in, 32)
                    pe.wait_ge(acc_ready, i * 3)
                    if s.attn:
                        pe.wait_ge(kt_ready, i - 1)
                    for n, a in enumerate((2, 0, 1)):
                        tok0 = acc_sb[:, 1 - p, a].rearrange("d (b n) -> d b n", b=GB)[:, :, 0]
                        mm = pe.matmul(bank[:, 0:GB], g1_sb[:, n, :], tok0, start=(n == 0), stop=(n == 2))
                    mm.then_inc(g1_done, 1)
                if t == 3 and s.prev:
                    pe.wait_ge(gprod_ready, i)
                    if s.prep:
                        pe.wait_ge(xt_ready, i + 2)
                    mm = pe.matmul(bank[:, 0:GB * 3], ones[:, :], gprod[:, :, :].rearrange("j b k -> j (b k)"),
                                   start=True, stop=True)
                    mm.then_inc(g2_done, 1)
                if t == 4 and s.attn:
                    pe.wait_ge(x3_ready, i - 1 + HEAD)
                    if s.prev:
                        pe.wait_ge(gprod_ready, i)
                    else:
                        pe.wait_ge(kt_ready, i - 1)
                    transposes(bank, lambda b: cols(x3, b), x3t_done)
                if t == 5 and s.prep:
                    pe.wait_ge(xt_ready, i + 2)
                    pe.wait_ge(w0_sel_in, (i + 2) * (16 * GB))
                    if s.prev:
                        pe.wait_ge(gsub_ready, i)
                    for b in range(GB):
                        mm = pe.matmul(cols(bank, b), w0_sel[:, b, :], cols(xT, b), start=True, stop=True)
                    mm.then_inc(l0_done, 1)
                if t == 6 and s.attn:
                    pe.wait_ge(qt_ready, i - 1)
                    pe.wait_ge(kt_ready, i - 1)
                    for b in range(GB):
                        mm = pe.matmul(cols(bank, b), cols(qT, b), cols(kT, b), start=True, stop=True)
                    mm.then_inc(qk_done, 1)
                if t == 7 and s.prev:
                    pe.wait_ge(mixed, i * 3)
                    if s.prep:
                        pe.wait_ge(x1_ready, i + 2)
                    transposes(bank, lambda b: cols(x2T, b), x2n_done)
                if t == 8 and s.prev:
                    pe.wait_ge(l2w_in, i * (32 * GB))
                    if s.attn:
                        pe.wait_ge(probs_ready, i - 1)
                    for b in range(GB):
                        mm = pe.matmul(cols(bank, b), wd_sel[:, b, :], cols(x2T, b), start=True, stop=True)
                    mm.then_inc(z_done, 1)
                if t == 9 and s.attn:
                    pe.wait_ge(probs_ready, i - 1)
                    if s.prev:
                        pe.wait_ge(x2n_ready, i)
                    transposes(bank, lambda b: cols(probs, b), pt_done)
                if t == 10 and s.prev:
                    pe.wait_ge(zt_ready, i)
                    for b in range(GB):
                        mm = pe.matmul(cols(bank, b), cols(zT, b), wu_sel[:, b, :], start=True, stop=True)
                    mm.then_inc(y_done, 1)
                if t == 11 and s.attn:
                    pe.wait_ge(pt_ready, i - 1)
                    for b in range(GB):
                        mm = pe.matmul(cols(bank, b), cols(pT, b), keys[:, p, b, :], start=True, stop=True)
                    mm.then_inc(pv_done, 1)

            def slot(s):
                for t in range(UNITS):
                    if s.mlp:
                        hidden(t, s)
                    if t >= 2 and s.mlp:
                        output(t - 2, s.i)
                    if t < 2 and s.prev:
                        output(t + UNITS - 2, s.i - 1)
                    piece(t, s)

            run_slots(pe, slot)

        @block.scalar
        def _(act):
            for half_ in range(2):
                act.wait_ge(w0t_done, half_ + 1)
                act.activation(w0_table[:, half_ * GB:(half_ + 1) * GB, :].rearrange("p s o -> p (s o)"),
                               misc[half_][:, :], ACT.Copy).then_inc(w0tab_ready, 1)

            def table_hi(n):
                act.wait_ge(stage_in[n], 32)
                act.activation(shared[:, n, 0], stage[:, n], ACT.Copy).then_inc(tab_hi, 1)

            def setup(i):
                if i == -1:
                    table_hi(0)
                    table_hi(1)

            def slot(s):
                i, p = s.i, s.p

                def relu_hi(k):
                    act.wait_ge(hid_done, i * UNITS + k + 1)
                    after(act, out_done, i * UNITS + k - 3)
                    hidden = hid_hi[:, k % 4] if k < NSH else hid_f[:, k - NSH]
                    act.activation(hidden, hid_ps[k % 3][:, :], ACT.Relu).then_inc(hi_ready, 1)

                def acc_out(a, g, q):
                    act.wait_ge(out_done, g * UNITS + (FC, 2 * FC, UNITS)[a])
                    if a == 0:
                        after(act, mixed, g * 3 - 3)
                    act.activation(acc_sb[:, q, a], acc_ps[a][:, :], ACT.Copy).then_inc(acc_ready, 1)

                for t in range(UNITS):
                    if s.mlp:
                        relu_hi(t)
                    if t == 0 and s.attn:
                        act.wait_ge(kt_done, i - 1)
                        after(act, qk_done, i - 2 + HEAD)
                        act.activation(kT[:, :], misc[0][:, :], ACT.Copy).then_inc(kt_ready, 1)
                    if t == 1 and s.prev:
                        acc_out(2, i - 1, 1 - p)
                    if t == 1 and s.prep:
                        act.wait_ge(xt_done, i + 2)
                        after(act, x1_ready, i + 1)
                        act.activation(xT[:, :], misc[1][:, :], ACT.Copy).then_inc(xt_ready, 1)
                    if t == 4 and s.prev:
                        act.wait_ge(gsub_ready, i)
                        act.activation(gexp[:, :, :], gsub[:, :, :], ACT.Exp).then_inc(gexp_ready, 1)
                    if t == 5 and s.mlp:
                        acc_out(0, i, p)
                    if t == 6 and s.prep:
                        act.wait_ge(x1_ready, i + 2)
                        act.activation(x1h[:, 1 - p], x1T[:, 1 - p], ACT.Copy).then_inc(x1h_ready, 1)
                    if t == 7 and s.attn:
                        act.wait_ge(negmax_ready, i - 1)
                        after(act, prec_ready, i - 2 + HEAD)
                        for b in range(GB):
                            op = act.activation(cols(probs, b), cols(misc[0], b), ACT.Exp, bias=negmax[:, b:b + 1],
                                                accum_out=psums[:, b:b + 1])
                        op.then_inc(probs_ready, 1)
                    if t == 7 and s.prev:
                        act.wait_ge(x2n_done, i)
                        after(act, x2nb_ready, i - 1)
                        act.activation(x2n[:, :], misc[1][:, :], ACT.Copy).then_inc(x2n_ready, 1)
                    if t == 8 and s.prev:
                        act.wait_ge(z_done, i)
                        act.wait_ge(bd_sel_ready, i)
                        after(act, y_done, i - 1)
                        for b in range(GB):
                            op = act.activation(cols(zT, b), cols(misc[0], b), ACT.Relu, bias=bd_sel[:, b:b + 1])
                        op.then_inc(zt_ready, 1)
                    if t == 9 and s.mlp:
                        acc_out(1, i, p)
                    if t == 9 and s.attn:
                        act.wait_ge(pt_done, i - 1)
                        act.activation(pT[:, :], misc[1][:, :], ACT.Copy).then_inc(pt_ready, 1)

            run_slots(act, slot, setup)

        @block.vector
        def _(dve):
            for s_ in (o_ready, prec_ready, x3_ready):
                dve.sem_inc(s_, HEAD)
            dve.wait_ge(consts, 4)
            dve.tensor_copy(row_f[:, :], row_i[:, :]).then_inc(rowf_ready, 1)
            dve.wait_ge(rowf_ready, 1)
            dve.wait_ge(idrows_in, 64)
            for n, rows in enumerate((P0, P2)):
                op = dve.tensor_scalar(onehot[0:rows, n, :], ids_rows[0:rows, n, :], row_f[0:rows, :], None, ALU.is_equal)
            op.then_inc(onehot_ready, 1)
            dve.wait_ge(cols_done, 1)
            dve.tensor_copy(columns[:, :, :].rearrange("p n b -> p (n b)"), hid_ps[0][:, 0:2 * B]).then_inc(cols_ready, 1)

            def table_lo(n):
                dve.wait_ge(tab_hi, n + 1)
                dve.tensor_tensor(shared[:, n, 1], stage[:, n], shared[:, n, 0].bitcast(F32),
                                  ALU.subtract).then_inc(tab_lo, 1)

            def setup(i):
                if i == -1:
                    table_lo(0)
                    table_lo(1)

            def per_batch(a):
                return a.unsqueeze(2).broadcast_to([128, GB, 3])

            def slot(s):
                i, p = s.i, s.p

                def relu_lo(k):
                    dve.wait_ge(hi_ready, i * UNITS + k + 1)
                    dve.scalar_tensor_tensor(out=hid_lo[:, k % 4], in0=hid_ps[k % 3][:, :], scalar=0.0,
                                             in1=hid_hi[:, k % 4].bitcast(F32), op0=ALU.max, op1=ALU.subtract).then_inc(lo_ready, 1)

                def mix(n):
                    src = x1T[:, 1 - p] if n == 0 else x2T[:, :]
                    for b in range(GB):
                        op = dve.scalar_tensor_tensor(out=cols(x2T, b), in0=cols(acc_sb[:, 1 - p, (2, 0, 1)[n]], b),
                                                      scalar=gate[:, b, n:n + 1], in1=cols(src, b), op0=ALU.mult, op1=ALU.add)
                    op.then_inc(mixed, 1)

                def ln_step(n, op):
                    op.then_inc(ln_steps, 1)
                    return (i - 2) * LN_STEPS + n

                def centered(b):
                    op = dve.scalar_tensor_tensor(out=cols(yg, b), in0=cols(y, b), scalar=meanvar[:, b, 0:1],
                                                  in1=g_sel[:, b, :], op0=ALU.subtract, op1=ALU.mult)
                    if b == GB - 1:
                        op.then_inc(yg_ready, 1)

                if s.attn:
                    dve.wait_ge(stats_ready, i - 1)
                for t in range(UNITS):
                    if s.mlp and t < NSH:
                        relu_lo(t)
                    if t == 0 and s.attn:
                        for b in range(GB):
                            op = dve.bn_aggr(meanvar[:, b, :], stats[:, b, :])
                        op.then_inc(meanvar_ready, 1)
                        dve.wait_ge(meanvar_ready, i - 1)
                        n = ln_step(1, dve.tensor_scalar(var[:, :], meanvar[:, :, 1], EPS, None, ALU.add))
                        dve.wait_ge(g_sel_ready, i - 1)
                        centered(0)
                        dve.wait_ge(ln_steps, n)
                        n = ln_step(2, dve.tensor_scalar(half[:, :], var[:, :].bitcast(I32), 1, None, ALU.arith_shift_right))
                        centered(1)
                        dve.wait_ge(ln_steps, n)
                        n = ln_step(3, dve.tensor_scalar(rstd[:, :].bitcast(I32), half[:, :], -1.0, RSQRT_MAGIC, ALU.mult, ALU.add))
                        centered(2)
                        for r in range(NEWTON):
                            dve.wait_ge(ln_steps, n)
                            n = ln_step(4 + 3 * r, dve.tensor_tensor(nt[:, 0], rstd[:, :], rstd[:, :], ALU.mult))
                            if r == 0:
                                centered(3)
                            dve.wait_ge(ln_steps, n)
                            n = ln_step(5 + 3 * r, dve.scalar_tensor_tensor(out=nt[:, 1], in0=nt[:, 0], scalar=-0.5, in1=var[:, :],
                                                                            op0=ALU.mult, op1=ALU.mult))
                            dve.wait_ge(ln_steps, n)
                            n = ln_step(6 + 3 * r, dve.scalar_tensor_tensor(out=rstd[:, :], in0=nt[:, 1], scalar=1.5, in1=rstd[:, :],
                                                                            op0=ALU.add, op1=ALU.mult))
                    if t == 1 and s.attn:
                        dve.wait_ge(ln_steps, (i - 1) * LN_STEPS)
                        dve.wait_ge(yg_ready, i - 1)
                        dve.wait_ge(x2nb_ready, i - 1)
                        after(dve, x3t_done, i - 2 + HEAD)
                        after(dve, o_ready, i - 2 + HEAD)
                        for b in range(GB):
                            op = dve.scalar_tensor_tensor(out=cols(x3, b), in0=cols(yg, b), scalar=rstd[:, b:b + 1],
                                                          in1=cols(x2nb, b), op0=ALU.mult, op1=ALU.add)
                        op.then_inc(x3_ready, 1)
                    if t == 2 and s.prev:
                        dve.wait_ge(g1_done, i)
                        after(dve, g2_done, i - 1)
                        dve.scalar_tensor_tensor(out=gprod[:, :, :], in0=per_batch(misc[0][:, 0:GB]), scalar=0.0,
                                                 in1=g2_sb[:, :].unsqueeze(1).broadcast_to([128, GB, 3]),
                                                 op0=ALU.max, op1=ALU.mult).then_inc(gprod_ready, 1)
                    if t == 3 and s.prev:
                        dve.wait_ge(g2_done, i)
                        logits = misc[1][:, 0:GB * 3].rearrange("p (b k) -> p b k", b=GB)
                        dve.tensor_reduce(gmax[:, :], logits, AX.X, ALU.max).then_inc(gmax_ready, 1)
                        dve.wait_ge(gmax_ready, i)
                        dve.tensor_tensor(gsub[:, :, :], logits, per_batch(gmax[:, :]), ALU.subtract).then_inc(gsub_ready, 1)
                    if t == 4 and s.prev:
                        dve.wait_ge(gexp_ready, i)
                        dve.tensor_reduce(gsum[:, :], gexp[:, :, :], AX.X, ALU.add).then_inc(gate_steps, 1)
                        dve.wait_ge(gate_steps, i * 3 - 2)
                        dve.reciprocal(grec[:, :], gsum[:, :]).then_inc(gate_steps, 1)
                        dve.wait_ge(gate_steps, i * 3 - 1)
                        dve.tensor_tensor(gate[:, :, :], gexp[:, :, :], per_batch(grec[:, :]), ALU.mult).then_inc(gate_steps, 1)
                    if t == 4 and s.attn:
                        dve.wait_ge(x3t_done, i - 1 + HEAD)
                        dve.wait_ge(em_sel_ready, i - 1)
                        dve.tensor_tensor(qT[:, :], misc[0][:, :], em_sel[:, :, :].rearrange("p b n -> p (b n)"),
                                          ALU.add).then_inc(qt_ready, 1)
                    if t == 4 and s.prev:
                        dve.wait_ge(gate_steps, i * 3)
                        dve.wait_ge(acc_ready, i * 3)
                        after(dve, z_done, i - 1)
                        mix(0)
                    if t == 5 and s.prep:
                        if s.prev:
                            dve.wait_ge(mixed, i * 3 - 2)
                        dve.wait_ge(l0_done, i + 2)
                        dve.wait_ge(b0_sel_ready, i + 2)
                        for b in range(GB):
                            op = dve.scalar_tensor_tensor(out=cols(x1T[:, 1 - p], b), in0=cols(misc[1], b),
                                                          scalar=b0_sel[:, b:b + 1], in1=cols(xT, b), op0=ALU.add, op1=ALU.add)
                        op.then_inc(x1_ready, 1)
                    if t == 5 and s.prev:
                        dve.wait_ge(mixed, i * 3 - 2)
                        mix(1)
                    if t == 6 and s.attn:
                        dve.wait_ge(qk_done, i - 1 + HEAD)
                        dve.tensor_reduce(negmax[:, :], misc[0][:, :].rearrange("p (b n) -> p b n", b=GB), AX.X, ALU.max,
                                          negate=True).then_inc(negmax_ready, 1)
                    if t == 6 and s.prev:
                        dve.wait_ge(mixed, i * 3 - 1)
                        mix(2)
                    if t == 8 and s.attn:
                        dve.wait_ge(probs_ready, i - 1)
                        dve.reciprocal(prec[:, :], psums[:, :]).then_inc(prec_ready, 1)
                    if t == 10 and s.prev:
                        dve.wait_ge(y_done, i)
                        dve.wait_ge(x2b_ready, i)
                        after(dve, yg_ready, i - 1)
                        dve.tensor_tensor(y[:, :], misc[0][:, :], x2b[:, :], ALU.add).then_inc(y_ready, 1)
                        dve.wait_ge(y_ready, i)
                        after(dve, meanvar_ready, i - 1)
                        for b in range(GB):
                            op = dve.bn_stats(stats[:, b, :], cols(y, b))
                        op.then_inc(stats_ready, 1)
                    if t == 11 and s.attn:
                        dve.wait_ge(pv_done, i - 1 + HEAD)
                        dve.wait_ge(prec_ready, i - 1 + HEAD)
                        after(dve, stored, i * 16 - 32 + 16 * HEAD)
                        for b in range(GB):
                            op = dve.scalar_tensor_tensor(out=cols(o_sb, b), in0=cols(misc[1], b), scalar=prec[:, b:b + 1],
                                                          in1=cols(x3, b), op0=ALU.mult, op1=ALU.add)
                        op.then_inc(o_ready, 1)

            run_slots(dve, slot, setup)

        @block.gpsimd
        def _(pool):
            pool.memset(ones[:, :], 1.0).then_inc(consts, 1)
            pool.memset(ident[:, :], 0.0).then_inc(consts, 1)
            pool.wait_ge(consts, 2)
            pool.affine_select(out=ident[:, :], in_=ident[:, :], compare_op=ALU.not_equal, fill=1.0,
                               base=0, pattern=[[-1, 128]], channel_multiplier=1).then_inc(consts, 1)
            pool.iota(row_i[:, :], [[0, 1]], base=0, channel_multiplier=1).then_inc(consts, 1)
            pool.wait_ge(cols_ready, 1)
            pool.wait_ge(ids_in, 64)
            pool.wait_ge(lntab_in, 64)

            def slot(s):
                i, p = s.i, s.p
                if s.prep:
                    after(pool, x1_ready, i + 1)
                    pool.tensor_copy(b0_sel[:, :], columns[:, 0, bass.ds((i * GB + GB) % B, GB)]).then_inc(b0_sel_ready, 1)
                if s.prev:
                    after(pool, zt_ready, i - 1)
                    pool.tensor_copy(bd_sel[:, :], columns[:, 1, bass.ds(i * GB - GB, GB)]).then_inc(bd_sel_ready, 1)
                if s.prev:
                    who = [pool.value_load(ids[0:1, 2, bass.ds(i * GB - GB + b, 1)], min_val=0, max_val=P2 - 1) for b in range(GB)]
                    stage5 = [pool.value_load(ids[0:1, 3, bass.ds(i * GB - GB + b, 1)], min_val=0, max_val=P3 - 1) for b in range(GB)]
                    up_b_, ln_g_, ln_b_ = [[ln_table[:, m, bass.ds(w_, 1), :].rearrange("p s d -> p (s d)") for w_ in who]
                                           for m in range(3)]
                    after(pool, yg_ready, i - 1)
                    for b in range(GB):
                        op = pool.tensor_copy(g_sel[:, b, :], ln_g_[b])
                    op.then_inc(g_sel_ready, 1)
                if s.prep:
                    pool.wait_ge(x1h_ready, i + 2)
                    pool.tensor_tensor(x1l[:, 1 - p], x1T[:, 1 - p], x1h[:, 1 - p].bitcast(F32),
                                       ALU.subtract).then_inc(x1l_ready, 1)
                if s.prev:
                    pool.wait_ge(x2n_ready, i)
                    after(pool, y_ready, i - 1)
                    for b in range(GB):
                        op = pool.tensor_tensor(cols(x2b, b), cols(x2n, b), up_b_[b], ALU.add)
                    op.then_inc(x2b_ready, 1)
                    after(pool, x3_ready, i - 1 + HEAD)
                    for b in range(GB):
                        op = pool.tensor_tensor(cols(x2nb, b), cols(x2n, b), ln_b_[b], ALU.add)
                    op.then_inc(x2nb_ready, 1)
                    after(pool, qt_ready, i - 1)
                    for b in range(GB):
                        op = pool.tensor_copy(em_sel[:, b, :], em_table[:, bass.ds(stage5[b], 1), :].rearrange("p s d -> p (s d)"))
                    op.then_inc(em_sel_ready, 1)

            run_slots(pool, slot)


_INS = ["x", "itok_B_0_7", "itok_B_0_2", "itok_B_0_6", "fside_BxSxS_0", "itok_B_0_5",
        "L0_cond_weight", "L0_cond_bias", "L1_cond_wi", "L1_cond_wo", "L1_cond_swi", "L1_cond_swo",
        "L1_cond_g1", "L1_cond_g2", "L2_cond_down_w", "L2_cond_down_b", "L2_cond_up_w", "L2_cond_up_b",
        "L2_cond_ln_g", "L2_cond_ln_b", "L3_cond_braak_embed"]


def kernel(**inputs):
    import numpy as _np
    import concourse.bacc as _bacc
    from concourse import mybir as _mybir
    from concourse.bass_utils import run_bass_kernel_spmd as _run

    nc = _bacc.Bacc("TRN2", target_bir_lowering=False, num_devices=1)
    arrays, args = {}, []
    for name in _INS:
        a = _np.ascontiguousarray(inputs[name])
        arrays[f"in_{name}_dram"] = a
        args.append(nc.dram_tensor(f"in_{name}_dram", a.shape, _mybir.dt.from_np(a.dtype), kind="ExternalInput").ap())
    shape = inputs["x"].shape
    args.append(nc.dram_tensor("out_0_dram", shape, _mybir.dt.float32, kind="ExternalOutput").ap())
    build(nc, *args)
    r = _run(nc, [arrays], core_ids=[0])
    return r.results[0]["out_0_dram"]
```

```python
from contextlib import ExitStack

import concourse.bass as bass
from concourse import mybir

F32 = mybir.dt.float32
F32R = mybir.dt.float32r
I32 = mybir.dt.int32
ALU = mybir.AluOpType
ACT = mybir.ActivationFunctionType
AX = mybir.AxisListType

GB = 4
UNIT = [(0, 0), (0, 1), 0, (0, 2), (0, 3), 1, (1, 0), (1, 1), 2, (1, 2), (1, 3), 3]
UNITS = len(UNIT)
NSH = 8
EPS = 1e-5
RSQRT_MAGIC = float(0x5F3759DF)
NEWTON = 3
HEAD = 1
LN_STEPS = 3 + 3 * NEWTON
WARM = 8
LOOP_FIRST, LOOP_LAST = 2, 7


def after(eng, sem, count):
    if isinstance(count, int) and count <= 0:
        return
    eng.wait_ge(sem, count)


def is_shared(t):
    return isinstance(UNIT[t], tuple)


def shared_until(t):
    return sum(is_shared(u) for u in range(t + 1))


def step_of(n):
    return [u for u in range(UNITS) if is_shared(u)][n]


class Slot:

    def __init__(self, i, p, h, prep, mlp, prev, attn):
        self.i, self.p, self.h = i, p, h
        self.prep = prep
        self.mlp = mlp
        self.prev = prev
        self.attn = attn


class Part:

    def __init__(self, n, parity, batches=range(GB), free=None, banks=None):
        self.n, self.parity, self.batches, self.banks = n, parity, batches, banks
        self.free = n - 1 if free is None else free
        self.small = slice(batches[0], batches[-1] + 1)
        self.cols = slice(batches[0] * 128, (batches[-1] + 1) * 128)

    def bank(self, piece):
        return self.banks[piece]


def run_slots(eng, body, before_slot=None, tail=None):
    for i, flags in ((-1, (1, 0, 0, 0)), (0, (1, 1, 0, 0)), (1, (1, 1, 1, 0))):
        if before_slot:
            before_slot(i)
        body(Slot(i, i % 2, i // 2, *flags))
    with eng.Fori(LOOP_FIRST // 2, (LOOP_LAST + 1) // 2) as pair:
        for p in range(2):
            body(Slot(pair * 2 + p, p, pair, 1, 1, 1, 1))
    tail()


def build(nc, x, id7, id2, id6, side, id5, w0, b0, wi, wo, swi, swo, g1, g2,
          down_w, down_b, up_w, up_b, ln_g, ln_b, embed, out):
    B, N, D = x.shape
    E, _, F = wi.shape
    P0, P2, P3 = w0.shape[0], down_w.shape[0], embed.shape[0]
    FC = F // D
    W = GB * N
    NG = B // GB
    RAW = F + FC * D
    assert N == D == 128 and W == 512 and FC == 4 and NG == 8

    with ExitStack() as ctx:
        def sb(name, shape, dt=F32):
            return ctx.enter_context(nc.sbuf_tensor(name, shape, dt))

        def sem(name):
            return ctx.enter_context(nc.semaphore(name))

        shared = sb("shared", [128, 2, 2, RAW], F32R)
        w0_table = sb("w0_table", [128, P0, 128])
        ln_table = sb("ln_table", [128, 3, P2, 128])
        em_table = sb("em_table", [128, P3, 128])
        columns = sb("columns", [128, 2, B])
        g1_sb = sb("g1_sb", [128, 3, 128])
        g2_sb = sb("g2_sb", [128, 3])
        ident = sb("ident", [128, 128])
        ones = sb("ones", [128, 128])
        ids = sb("ids", [1, 4, B], I32)
        stage = sb("stage", [128, 2, RAW])
        w0_raw = sb("w0_raw", [128, P0, 128])
        ids_rows = sb("ids_rows", [P0, 2, B], I32)
        row_i = sb("row_i", [P0, 1], I32)
        row_f = sb("row_f", [P0, 1])
        onehot = sb("onehot", [P0, 2, B])
        bias_rows = sb("bias_rows", [P0, 2, 128])
        esel = sb("esel", [128, GB, RAW])
        w0_sel = sb("w0_sel", [128, GB, 128])
        wd_sel = sb("wd_sel", [128, GB, 128])
        wu_sel = sb("wu_sel", [128, GB, 128])
        b0_sel = sb("b0_sel", [128, GB])
        bd_sel = sb("bd_sel", [128, GB])
        g_sel = sb("g_sel", [128, GB, 128])
        em_sel = sb("em_sel", [128, GB, 128])
        xin = sb("xin", [128, 2, GB, 128])
        keys = sb("keys", [128, 2, GB, 128])
        xT = sb("xT", [128, W])
        x1T = sb("x1T", [128, 2, W])
        x1h = sb("x1h", [128, 2, W], F32R)
        x1l = sb("x1l", [128, 2, W], F32R)
        hid_hi = sb("hid_hi", [128, 4, W], F32R)
        hid_lo = sb("hid_lo", [128, 4, W], F32R)
        hid_f = sb("hid_f", [128, GB, W])
        acc_sb = sb("acc_sb", [128, 2, 3, W])
        gprod = sb("gprod", [128, GB, 3])
        gmax = sb("gmax", [128, GB])
        gsub = sb("gsub", [128, GB, 3])
        gexp = sb("gexp", [128, GB, 3])
        gsum = sb("gsum", [128, GB])
        grec = sb("grec", [128, GB])
        gate = sb("gate", [128, GB, 3])
        scaled = sb("scaled", [128, 3, W // 2])
        x2T = sb("x2T", [128, W])
        x2n = sb("x2n", [128, W])
        x2b = sb("x2b", [128, W])
        zT = sb("zT", [128, W])
        y = sb("y", [128, W])
        stats = sb("stats", [128, GB, 6])
        meanvar = sb("meanvar", [128, GB, 2])
        var = sb("var", [128, GB])
        half = sb("half", [128, GB], I32)
        rstd = sb("rstd", [128, GB])
        nt = sb("nt", [128, 2, GB])
        yg = sb("yg", [128, W])
        x2nb = sb("x2nb", [128, W])
        x3 = sb("x3", [128, 2, W])
        qT = sb("qT", [128, W])
        kT = sb("kT", [128, 2, W])
        negmax = sb("negmax", [128, GB])
        probs = sb("probs", [128, W])
        psums = sb("psums", [128, GB])
        prec = sb("prec", [128, GB])
        pT = sb("pT", [128, W])
        o_sb = sb("o_sb", [128, 2, W])

        hid_ps = [ctx.enter_context(nc.psum_tensor(f"hid_ps{n}", [128, W], F32)) for n in range(3)]
        acc_ps = [ctx.enter_context(nc.psum_tensor(f"acc_ps{n}", [128, W], F32)) for n in range(3)]
        misc = [ctx.enter_context(nc.psum_tensor(f"misc{n}", [128, W], F32)) for n in range(2)]

        GATE_BANKS = hid_ps[0], hid_ps[1]
        HALVES = [dict(X2N=b_[0], Z=b_[1], Y=b_[2], X3T=b_[0], QK=b_[1], PT=b_[2], PV=b_[0]) for b_ in (hid_ps, acc_ps)]
        LAST = [Part(NG + h, 1, range(h * GB // 2, (h + 1) * GB // 2), NG - 1, HALVES[h]) for h in range(2)]
        QUARTER = dict(X3T=misc[0], QK=hid_ps[1], PT=hid_ps[2], PV=misc[0])
        LAST_L3 = [LAST[0]] + [Part(NG - 1 + b, 1, range(b, b + 1), NG - 1, banks) for b, banks in ((2, HALVES[1]), (3, QUARTER))]

        ids_in = sem("ids_in")
        idrows_in = sem("idrows_in")
        w0_in = sem("w0_in")
        gates_in = sem("gates_in")
        lntab_in = sem("lntab_in")
        id7_in = sem("id7_in")
        w0_first_ready = sem("w0_first_ready")
        x1_half_ready, x1h_half_ready = sem("x1_half_ready"), sem("x1h_half_ready")
        stage_in = [sem(f"stage_in{n}") for n in range(4)]
        consts = sem("consts")
        w0t_done = sem("w0t_done")
        w0tab_ready = sem("w0tab_ready")
        rowf_ready = sem("rowf_ready")
        onehot_ready = sem("onehot_ready")
        cols_done = sem("cols_done")
        cols_ready = sem("cols_ready")
        tab_hi = sem("tab_hi")
        tab_lo = sem("tab_lo")
        x_in = [sem("x_in0"), sem("x_in1")]
        k_in = [sem("k_in0"), sem("k_in1")]
        w0_sel_in = sem("w0_sel_in")
        l2w_in = sem("l2w_in")
        esel_in = [sem(f"esel_in{b}") for b in range(GB)]
        stored = sem("stored")
        hid_done = sem("hid_done")
        out_done = sem("out_done")
        kt_done, xt_done, g1_done, x3t_done = sem("kt_done"), sem("xt_done"), sem("g1_done"), sem("x3t_done")
        g2_done, qk_done, l0_done, pt_done = sem("g2_done"), sem("qk_done"), sem("l0_done"), sem("pt_done")
        x2n_done, z_done, pv_done, y_done = sem("x2n_done"), sem("z_done"), sem("pv_done"), sem("y_done")
        hi_ready = sem("hi_ready")
        acc_ready = sem("acc_ready")
        kt_ready, xt_ready = sem("kt_ready"), sem("xt_ready")
        gexp_ready, probs_ready, x1h_ready = sem("gexp_ready"), sem("probs_ready"), sem("x1h_ready")
        pt_ready, x2n_ready, zt_ready = sem("pt_ready"), sem("x2n_ready"), sem("zt_ready")
        lo_ready = sem("lo_ready")
        gprod_ready, gmax_ready, gsub_ready = sem("gprod_ready"), sem("gmax_ready"), sem("gsub_ready")
        gate_steps, mixed = sem("gate_steps"), sem("mixed")
        negmax_ready, x1_ready, prec_ready = sem("negmax_ready"), sem("x1_ready"), sem("prec_ready")
        o_ready, y_ready = sem("o_ready"), sem("y_ready")
        stats_ready, meanvar_ready = sem("stats_ready"), sem("meanvar_ready")
        ln_steps, yg_ready = sem("ln_steps"), sem("yg_ready")
        ln_steps_last = sem("ln_steps_last")
        x3_ready, qt_ready = sem("x3_ready"), sem("qt_ready")
        scaled_ready, mixed_last = sem("scaled_ready"), sem("mixed_last")
        b0_sel_ready, bd_sel_ready = sem("b0_sel_ready"), sem("bd_sel_ready")
        x2nb_ready, g_sel_ready, em_sel_ready = sem("x2nb_ready"), sem("g_sel_ready"), sem("em_sel_ready")
        x1l_ready, x2b_ready = sem("x1l_ready"), sem("x2b_ready")

        block = ctx.enter_context(nc.Block())

        def cols(t, b):
            return t[:, b * 128:(b + 1) * 128]

        @block.sync
        def _(sp):
            sp.sem_inc(stored, 16 * HEAD)

            def load_x(g, p):
                first = (g * GB) % B
                sp.dma_start(xin[:, p], x[bass.ds(first, GB)].rearrange("b n d -> n b d")).then_inc(x_in[p], 16)

            def load_w0(g):
                for b in range(GB):
                    who = sp.value_load(ids[0:1, 0, bass.ds((g * GB + b) % B, 1)], min_val=0, max_val=P0 - 1)
                    sp.dma_start(w0_sel[:, b, :], w0_table[:, bass.ds(who, 1), :]).then_inc(w0_sel_in, 16)

            def load_ids(n, t):
                sp.dma_start(ids[0:1, n, :], t.rearrange("(a b) -> a b", a=1)).then_inc(id7_in if n == 0 else ids_in, 16)

            def load_bias(n, ids_, bias, rows):
                sp.dma_start(ids_rows[0:rows, n, :], ids_.partition_broadcast(rows)).then_inc(idrows_in, 16)
                sp.dma_start(bias_rows[0:rows, n, :], bias).then_inc(idrows_in, 16)

            def load_stage(e):
                sp.dma_start(stage[:, e, 0:F], swi[e]).then_inc(stage_in[2 * e], 16)
                sp.dma_start(stage[:, e, F:RAW].rearrange("p (c d) -> p c d", c=FC),
                             swo[e].rearrange("(c p) d -> p c d", p=128)).then_inc(stage_in[2 * e + 1], 16)

            load_ids(0, id7)
            sp.dma_start(w0_raw[:, :, :], w0.rearrange("s o h -> o s h")).then_inc(w0_in, 16)
            load_x(0, 0)
            load_bias(0, id7, b0, P0)
            load_bias(1, id6, down_b, P2)
            load_stage(0)
            for n, t in ((1, id2), (2, id6), (3, id5)):
                load_ids(n, t)
            load_stage(1)
            sp.wait_ge(id7_in, 16)
            sp.wait_ge(ids_in, 48)

            def load_expert(g, b):
                after(sp, out_done, (g - 1) * UNITS + UNIT.index(b) + 1)
                who = sp.value_load(ids[0:1, 1, bass.ds((g * GB + b) % B, 1)], min_val=0, max_val=E - 1)
                sp.dma_start(esel[:, b, 0:F], wi[bass.ds(who, 1)].rearrange("e d f -> (e d) f")).then_inc(esel_in[b], 16)
                sp.dma_start(esel[:, b, F:RAW].rearrange("p (c d) -> p c d", c=FC),
                             wo[bass.ds(who, 1)].rearrange("e (c p) d -> p (e c) d", p=128)).then_inc(esel_in[b], 16)

            def load_tables(i):
                if i == 0:
                    load_expert(0, 3)
                    sp.dma_start(g1_sb[:, :, :], g1.rearrange("(c p) j -> p c j", p=128)).then_inc(gates_in, 16)
                    sp.dma_start(g2_sb[:, :], g2).then_inc(gates_in, 16)
                    for n, t in enumerate((up_b, ln_g, ln_b)):
                        sp.dma_start(ln_table[:, n], t.partition_broadcast(128)).then_inc(lntab_in, 16)
                    sp.dma_start(em_table[:, :, :], embed.partition_broadcast(128)).then_inc(lntab_in, 16)

            def load_l2(i):
                who = [sp.value_load(ids[0:1, 2, bass.ds(i * GB + b, 1)], min_val=0, max_val=P2 - 1) for b in range(GB)]
                after(sp, y_done, i)
                for b in range(GB):
                    sp.dma_start(wd_sel[:, b, :], down_w[bass.ds(who[b], 1)].rearrange("s h k -> (s h) k")).then_inc(l2w_in, 16)
                for b in range(GB):
                    sp.dma_start(wu_sel[:, b, :], up_w[bass.ds(who[b], 1)].rearrange("s k h -> (s k) h")).then_inc(l2w_in, 16)

            def load_keys(i, p):
                after(sp, pv_done, i - 2 + HEAD)
                sp.dma_start(keys[:, 1 - p], side[bass.ds(i * GB - GB, GB)].rearrange("b n d -> n b d")).then_inc(k_in[1 - p], 16)

            def store(part, batch):
                sp.wait_ge(o_ready, part.n + HEAD)
                count = len(part.batches)
                sp.dma_start(out[bass.ds(batch, count)].rearrange("b n d -> n b d"),
                             o_sb[:, part.parity, part.cols].rearrange("n (b d) -> n b d", b=count)).then_inc(stored, 16)

            def slot(s):
                i, p, h = s.i, s.p, s.h
                if s.mlp and not (isinstance(i, int) and i == 0):
                    load_expert(i, 3)
                if s.prev:
                    load_keys(i, p)
                if s.prep:
                    after(sp, xt_done, i + 1)
                    load_x(i + 2, p)
                    load_expert(i + 1, 0)
                    load_expert(i + 1, 1)
                    after(sp, l0_done, i + 2)
                    load_w0(i + 2)
                    load_expert(i + 1, 2)
                if s.mlp:
                    load_l2(i)
                if s.attn:
                    store(Part(i - 1, p), i * GB - 2 * GB)

            def tail():
                load_keys(NG, NG % 2)
                sp.wait_ge(stored, 16 * (NG - 2 + HEAD))
                store(Part(NG - 1, 0), B - 2 * GB)
                for part in LAST_L3:
                    store(part, B - GB + part.batches[0])

            run_slots(sp, slot, load_tables, tail)
            sp.wait_ge(x_in[0], 16 * (NG // 2 + 1))
            sp.wait_ge(x_in[1], 16 * (NG // 2 + 1))
            sp.wait_ge(w0_sel_in, 16 * GB * (NG + 1))
            for b in range(GB - 1):
                sp.wait_ge(esel_in[b], 32 * (NG + 1))
            sp.wait_ge(stored, 16 * (NG - 1 + len(LAST_L3) + HEAD))

        @block.tensor
        def _(pe):
            for s_ in (qk_done, x3t_done, pv_done):
                pe.sem_inc(s_, HEAD)

            def transposes(bank, src, done):
                for b in range(GB):
                    mm = pe.transpose(cols(bank, b), src(b), ident[:, :])
                mm.then_inc(done, 1)

            def keep_warm(n, bank=hid_ps[2]):
                for _ in range(n):
                    pe.matmul(bank[:, 0:128], ones[:, :], ones[:, :], start=True, stop=True)

            pe.wait_ge(consts, 3)
            keep_warm(6)
            pe.wait_ge(w0_in, 16)
            for half_ in range(2):
                transposes(acc_ps[half_], lambda b: w0_raw[:, half_ * GB + b, :], w0t_done)

            def bias_columns():
                pe.wait_ge(idrows_in, 64)
                pe.wait_ge(onehot_ready, 1)
                for n, rows in enumerate((P0, P2)):
                    mm = pe.matmul(hid_ps[0][:, n * B:(n + 1) * B], bias_rows[0:rows, n, :], onehot[0:rows, n, :],
                                   start=True, stop=True)
                mm.then_inc(cols_done, 1)

            def hidden(k, s):
                i, p = s.i, s.p
                bank = hid_ps[k % 3]
                if k == 0:
                    pe.wait_ge(x1h_ready, i + 1)
                    pe.wait_ge(x1l_ready, i + 1)
                    if isinstance(i, int) and i == 0:
                        pe.wait_ge(cols_ready, 1)
                g, was = (i, k - 3) if k >= 3 else (i - 1, k - 3 + UNITS)
                if is_shared(was):
                    after(pe, lo_ready, g * NSH + shared_until(was))
                else:
                    after(pe, hi_ready, g * UNITS + was + 1)
                if is_shared(k):
                    e, c = UNIT[k]
                    if isinstance(i, int) and i == 0 and c == 0:
                        pe.wait_ge(tab_lo, 2 * e + 1)
                    w_hi, w_lo = cols(shared[:, e, 0], c), cols(shared[:, e, 1], c)
                    pe.matmul(bank[:, :], w_hi, x1h[:, p], start=True, stop=False)
                    pe.matmul(bank[:, :], w_lo, x1h[:, p], start=False, stop=False)
                    mm = pe.matmul(bank[:, :], w_hi, x1l[:, p], start=False, stop=True)
                else:
                    b = UNIT[k]
                    pe.wait_ge(esel_in[b], i * 32 + 32)
                    for c in range(FC):
                        mm = pe.matmul(cols(bank, c), cols(esel[:, b], c), cols(x1T[:, p], b), start=True, stop=True)
                mm.then_inc(hid_done, 1)

            def output(k, i):
                if is_shared(k):
                    e, c = UNIT[k]
                    n = shared_until(k)
                    pe.wait_ge(lo_ready, i * NSH + n)
                    h_hi, h_lo = hid_hi[:, (n - 1) % 4], hid_lo[:, (n - 1) % 4]
                    if isinstance(i, int) and i == 0 and c == 0:
                        pe.wait_ge(tab_lo, 2 * e + 2)
                        pe.wait_ge(w0tab_ready, 2)
                    if c == 0:
                        after(pe, acc_ready, i * 3 - 2 + e)
                    w_hi, w_lo = cols(shared[:, e, 0], FC + c), cols(shared[:, e, 1], FC + c)
                    pe.matmul(acc_ps[e][:, :], w_hi, h_hi, start=(c == 0), stop=False)
                    pe.matmul(acc_ps[e][:, :], w_lo, h_hi, start=False, stop=False)
                    mm = pe.matmul(acc_ps[e][:, :], w_hi, h_lo, start=False, stop=(c == FC - 1))
                else:
                    b = UNIT[k]
                    pe.wait_ge(hi_ready, i * UNITS + k + 1)
                    if b == 0:
                        after(pe, acc_ready, i * 3)
                    for c in range(FC):
                        mm = pe.matmul(cols(acc_ps[2], b), cols(esel[:, b], FC + c), cols(hid_f[:, b], c),
                                       start=(c == 0), stop=(c == FC - 1))
                mm.then_inc(out_done, 1)

            def gate1(i, q, bank):
                if isinstance(i, int) and i == 1:
                    pe.wait_ge(gates_in, 32)
                pe.wait_ge(acc_ready, i * 3)
                for n, a in enumerate((2, 0, 1)):
                    tok0 = acc_sb[:, q, a].rearrange("d (b n) -> d b n", b=GB)[:, :, 0]
                    mm = pe.matmul(bank[:, 0:GB], g1_sb[:, n, :], tok0, start=(n == 0), stop=(n == 2))
                mm.then_inc(g1_done, 1)

            def gate2(i, bank):
                pe.wait_ge(gprod_ready, i)
                mm = pe.matmul(bank[:, 0:GB * 3], ones[:, :], gprod[:, :, :].rearrange("j b k -> j (b k)"),
                               start=True, stop=True)
                mm.then_inc(g2_done, 1)

            def piece(t, s):
                i, p, h = s.i, s.p, s.h
                bank = misc[t % 2]
                if t == 0 and s.attn:
                    pe.wait_ge(k_in[p], h * 16)
                    after(pe, y_ready, i - 1)
                    transposes(bank, lambda b: keys[:, p, b, :], kt_done)
                if t == 1 and s.prep:
                    pe.wait_ge(x_in[1 - p], (h + 1 + p) * 16)
                    after(pe, o_ready, i - 2 + HEAD)
                    transposes(bank, lambda b: xin[:, 1 - p, b, :], xt_done)
                if t == 2 and s.prev:
                    if s.attn:
                        pe.wait_ge(kt_ready, i - 1)
                    gate1(i, 1 - p, bank)
                if t == 3 and s.prev:
                    if s.prep:
                        pe.wait_ge(xt_ready, i + 2)
                    gate2(i, bank)
                if t == 4 and s.attn:
                    pe.wait_ge(x3_ready, i - 1 + HEAD)
                    if s.prev:
                        pe.wait_ge(gprod_ready, i)
                    else:
                        pe.wait_ge(kt_ready, i - 1)
                    transposes(bank, lambda b: cols(x3[:, p], b), x3t_done)
                if t == 5 and s.attn:
                    pe.wait_ge(qt_ready, i - 1)
                    pe.wait_ge(kt_ready, i - 1)
                    if s.prev:
                        pe.wait_ge(gsub_ready, i)
                    for b in range(GB):
                        mm = pe.matmul(cols(bank, b), cols(qT, b), cols(kT[:, p], b), start=True, stop=True)
                    mm.then_inc(qk_done, 1)
                if t == 6 and s.prep:
                    pe.wait_ge(xt_ready, i + 2)
                    if isinstance(i, int) and i == -1:
                        bias_columns()
                        pe.wait_ge(w0_first_ready, 1)
                    after(pe, w0_sel_in, (i + 1) * (16 * GB))
                    if s.attn:
                        pe.wait_ge(qt_ready, i - 1)
                    elif s.prev:
                        pe.wait_ge(gprod_ready, i)
                    for b in range(GB):
                        mm = pe.matmul(cols(bank, b), w0_sel[:, b, :], cols(xT, b), start=True, stop=True)
                    mm.then_inc(l0_done, 1)
                if t == 7 and s.prev:
                    pe.wait_ge(mixed, i * 3)
                    if s.attn:
                        pe.wait_ge(probs_ready, i - 1)
                    transposes(bank, lambda b: cols(x2T, b), x2n_done)
                if t == 8 and s.prev:
                    pe.wait_ge(l2w_in, i * (32 * GB))
                    if s.prep:
                        pe.wait_ge(x1_ready, i + 2)
                    for b in range(GB):
                        mm = pe.matmul(cols(bank, b), wd_sel[:, b, :], cols(x2T, b), start=True, stop=True)
                    mm.then_inc(z_done, 1)
                if t == 9 and s.attn:
                    pe.wait_ge(probs_ready, i - 1)
                    if s.prev:
                        pe.wait_ge(x2n_ready, i)
                    transposes(bank, lambda b: cols(probs, b), pt_done)
                if t == 10 and s.prev:
                    pe.wait_ge(zt_ready, i)
                    for b in range(GB):
                        mm = pe.matmul(cols(bank, b), cols(zT, b), wu_sel[:, b, :], start=True, stop=True)
                    mm.then_inc(y_done, 1)
                if t == 11 and s.attn:
                    pe.wait_ge(pt_ready, i - 1)
                    for b in range(GB):
                        mm = pe.matmul(cols(bank, b), cols(pT, b), keys[:, p, b, :], start=True, stop=True)
                    mm.then_inc(pv_done, 1)

            def slot(s):
                for t in range(UNITS):
                    if s.mlp:
                        hidden(t, s)
                    if t >= 2 and s.mlp:
                        output(t - 2, s.i)
                    if t < 2 and s.prev:
                        output(t + UNITS - 2, s.i - 1)
                    piece(t, s)

            def warm_up(i):
                if i == 0:
                    keep_warm(WARM)

            def last_transposes(part, name, src, done):
                for b in part.batches:
                    mm = pe.transpose(cols(part.bank(name), b), cols(src, b), ident[:, :])
                mm.then_inc(done, 1)

            def last_products(part, name, left, right, done):
                for b in part.batches:
                    mm = pe.matmul(cols(part.bank(name), b), left(b), right(b), start=True, stop=True)
                mm.then_inc(done, 1)

            def last_down(part):
                if part is LAST[0]:
                    pe.wait_ge(mixed, part.n * 3)
                else:
                    pe.wait_ge(mixed_last, 3)
                last_transposes(part, "X2N", x2T, x2n_done)
                pe.wait_ge(l2w_in, NG * (32 * GB))
                last_products(part, "Z", lambda b: wd_sel[:, b, :], lambda b: cols(x2T, b), z_done)

            def last_up(part):
                pe.wait_ge(zt_ready, part.n)
                last_products(part, "Y", lambda b: cols(zT, b), lambda b: wu_sel[:, b, :], y_done)

            def last_x3t(part):
                pe.wait_ge(x3_ready, part.n + HEAD)
                last_transposes(part, "X3T", x3[:, 1], x3t_done)

            def last_qk(part):
                pe.wait_ge(qt_ready, part.n)
                pe.wait_ge(kt_ready, NG)
                last_products(part, "QK", lambda b: cols(qT, b), lambda b: cols(kT[:, 1], b), qk_done)

            def last_pt(part):
                pe.wait_ge(probs_ready, part.n)
                last_transposes(part, "PT", probs, pt_done)

            def last_pv(part):
                pe.wait_ge(pt_ready, part.n)
                last_products(part, "PV", lambda b: cols(pT, b), lambda b: keys[:, 1, b, :], pv_done)

            def tail():
                before, (first, second), (_, third, fourth) = Slot(NG, 0, NG // 2, 0, 0, 0, 1), LAST, LAST_L3
                output(UNITS - 2, NG - 1)
                piece(0, before)
                output(UNITS - 1, NG - 1)
                keep_warm(4)
                gate1(NG, 1, GATE_BANKS[0])
                keep_warm(2)
                gate2(NG, GATE_BANKS[1])
                keep_warm(12)
                last_down(first)
                piece(4, before)
                last_up(first)
                last_down(second)
                piece(5, before)
                pe.wait_ge(k_in[1], (NG // 2) * 16)
                transposes(misc[0], lambda b: keys[:, 1, b, :], kt_done)
                last_up(second)
                keep_warm(3, hid_ps[0])
                piece(9, before)
                keep_warm(1, hid_ps[0])
                last_x3t(first)
                piece(11, before)
                last_qk(first)
                keep_warm(5, acc_ps[0])
                last_x3t(third)
                last_pt(first)
                last_x3t(fourth)
                last_qk(third)
                last_qk(fourth)
                last_pv(first)
                last_pt(third)
                last_pt(fourth)
                last_pv(third)
                last_pv(fourth)

            run_slots(pe, slot, warm_up, tail)

        @block.scalar
        def _(act):
            act.wait_ge(w0t_done, 1)
            act.activation(w0_table[:, 0:GB, :].rearrange("p s o -> p (s o)"), acc_ps[0][:, :], ACT.Copy).then_inc(w0tab_ready, 1)

            def table_hi(n):
                e, part = n // 2, slice(n % 2 * F, n % 2 * F + F)
                act.wait_ge(stage_in[n], 16)
                act.activation(shared[:, e, 0, part], stage[:, e, part], ACT.Copy).then_inc(tab_hi, 1)

            def acc_out(a, g, q):
                act.wait_ge(out_done, g * UNITS + (step_of(FC - 1) + 1, step_of(NSH - 1) + 1, UNITS)[a])
                if a == 0:
                    after(act, mixed, g * 3 - 3)
                act.activation(acc_sb[:, q, a], acc_ps[a][:, :], ACT.Copy).then_inc(acc_ready, 1)

            def gate_exp(i):
                act.wait_ge(gsub_ready, i)
                act.activation(gexp[:, :, :], gsub[:, :, :], ACT.Exp).then_inc(gexp_ready, 1)

            def keys_out(n, q, bank):
                act.wait_ge(kt_done, n)
                act.activation(kT[:, q], bank[:, :], ACT.Copy).then_inc(kt_ready, 1)

            def probabilities(part, bank):
                act.wait_ge(negmax_ready, part.n)
                after(act, prec_ready, part.free + HEAD)
                for b in part.batches:
                    op = act.activation(cols(probs, b), cols(bank, b), ACT.Exp, bias=negmax[:, b:b + 1],
                                        accum_out=psums[:, b:b + 1])
                op.then_inc(probs_ready, 1)

            def x2n_out(part, bank):
                act.wait_ge(x2n_done, part.n)
                after(act, x2nb_ready, part.free)
                act.activation(x2n[:, part.cols], bank[:, part.cols], ACT.Copy).then_inc(x2n_ready, 1)

            def relu_z(part, bank):
                act.wait_ge(z_done, part.n)
                act.wait_ge(bd_sel_ready, part.free + 1)
                after(act, y_done, part.free)
                for b in part.batches:
                    op = act.activation(cols(zT, b), cols(bank, b), ACT.Relu, bias=bd_sel[:, b:b + 1])
                op.then_inc(zt_ready, 1)

            def pt_out(part, bank):
                act.wait_ge(pt_done, part.n)
                act.activation(pT[:, part.cols], bank[:, part.cols], ACT.Copy).then_inc(pt_ready, 1)

            def slot(s):
                i, p = s.i, s.p
                l2, l3 = Part(i, 1 - p), Part(i - 1, p)

                def relu_hi(k):
                    act.wait_ge(hid_done, i * UNITS + k + 1)
                    if is_shared(k):
                        n = shared_until(k) - 1
                        hidden = hid_hi[:, n % 4]
                        after(act, out_done, i * UNITS + step_of(n - 4) + 1 - (0 if n >= 4 else UNITS))
                    else:
                        hidden = hid_f[:, UNIT[k]]
                        after(act, out_done, (i - 1) * UNITS + k + 1)
                    act.activation(hidden, hid_ps[k % 3][:, :], ACT.Relu).then_inc(hi_ready, 1)

                for t in range(UNITS):
                    if t == 4 and s.prev:
                        gate_exp(i)
                    if s.mlp:
                        relu_hi(t)
                    if t == 0 and s.prev:
                        acc_out(1, i - 1, 1 - p)
                    if t == 0 and s.attn:
                        after(act, qk_done, i - 2 + HEAD)
                        keys_out(i - 1, p, misc[0])
                    if t == 1 and s.prev:
                        acc_out(2, i - 1, 1 - p)
                    if t == 1 and s.prep:
                        act.wait_ge(xt_done, i + 2)
                        after(act, x1_ready, i + 1)
                        act.activation(xT[:, :], misc[1][:, :], ACT.Copy).then_inc(xt_ready, 1)
                        if isinstance(i, int) and i == -1:
                            table_hi(0)
                    if t == 6 and s.mlp:
                        acc_out(0, i, p)
                    if t == 6 and s.attn:
                        probabilities(l3, misc[1])
                    if t == 7 and s.prev:
                        x2n_out(l2, misc[1])
                    if t == 8 and s.prep:
                        if isinstance(i, int) and i == -1:
                            act.wait_ge(x1_half_ready, 1)
                            act.activation(x1h[:, 0, 0:W // 2], x1T[:, 0, 0:W // 2], ACT.Copy).then_inc(x1h_half_ready, 1)
                            act.wait_ge(x1_ready, 1)
                            act.activation(x1h[:, 0, W // 2:W], x1T[:, 0, W // 2:W], ACT.Copy).then_inc(x1h_ready, 1)
                        else:
                            act.wait_ge(x1_ready, i + 2)
                            act.activation(x1h[:, 1 - p], x1T[:, 1 - p], ACT.Copy).then_inc(x1h_ready, 1)
                        if isinstance(i, int) and i == -1:
                            for n in range(1, 4):
                                table_hi(n)
                    if t == 8 and s.prev:
                        relu_z(l2, misc[0])
                    if t == 9 and s.attn:
                        pt_out(l3, misc[1])

            def tail():
                before, (first, second), (_, third, fourth) = Part(NG - 1, 0), LAST, LAST_L3
                acc_out(1, NG - 1, 1)
                keys_out(NG - 1, 0, misc[0])
                acc_out(2, NG - 1, 1)
                gate_exp(NG)
                act.wait_ge(gate_steps, NG * 3)
                for n in range(3):
                    for b in second.batches:
                        op = act.activation(cols(scaled[:, n], b - second.batches[0]), cols(acc_sb[:, 1, (2, 0, 1)[n]], b),
                                            ACT.Copy, scale=gate[:, b, n:n + 1])
                    op.then_inc(scaled_ready, 1)
                x2n_out(first, first.bank("X2N"))
                relu_z(first, first.bank("Z"))
                x2n_out(second, second.bank("X2N"))
                relu_z(second, second.bank("Z"))
                keys_out(NG, 1, misc[0])
                probabilities(before, misc[1])
                pt_out(before, misc[1])
                probabilities(first, first.bank("QK"))
                pt_out(first, first.bank("PT"))
                probabilities(third, third.bank("QK"))
                probabilities(fourth, fourth.bank("QK"))
                pt_out(third, third.bank("PT"))
                pt_out(fourth, fourth.bank("PT"))

            run_slots(act, slot, tail=tail)

        @block.vector
        def _(dve):
            for s_ in (o_ready, prec_ready, x3_ready):
                dve.sem_inc(s_, HEAD)
            dve.wait_ge(consts, 4)
            dve.tensor_copy(row_f[:, :], row_i[:, :]).then_inc(rowf_ready, 1)
            dve.wait_ge(id7_in, 16)
            first = [dve.value_load(ids[0:1, 0, b:b + 1], min_val=0, max_val=P0 - 1) for b in range(GB)]
            dve.wait_ge(rowf_ready, 1)
            dve.wait_ge(idrows_in, 64)
            for n, rows in enumerate((P0, P2)):
                op = dve.tensor_scalar(onehot[0:rows, n, :], ids_rows[0:rows, n, :], row_f[0:rows, :], None, ALU.is_equal)
            op.then_inc(onehot_ready, 1)
            dve.wait_ge(w0t_done, 2)
            dve.tensor_copy(w0_table[:, GB:2 * GB, :].rearrange("p s o -> p (s o)"), acc_ps[1][:, :]).then_inc(w0tab_ready, 1)
            def table_lo(n):
                e, part = n // 2, slice(n % 2 * F, n % 2 * F + F)
                dve.wait_ge(tab_hi, n + 1)
                dve.tensor_tensor(shared[:, e, 1, part], stage[:, e, part], shared[:, e, 0, part].bitcast(F32),
                                  ALU.subtract).then_inc(tab_lo, 1)

            dve.wait_ge(w0tab_ready, 2)
            for b in range(GB):
                op = dve.tensor_copy(w0_sel[:, b, :], w0_table[:, bass.ds(first[b], 1), :].rearrange("p s o -> p (s o)"))
            op.then_inc(w0_first_ready, 1)
            dve.wait_ge(cols_done, 1)
            dve.tensor_copy(columns[:, :, :].rearrange("p n b -> p (n b)"), hid_ps[0][:, 0:2 * B]).then_inc(cols_ready, 1)
            table_lo(0)

            def per_batch(a):
                return a.unsqueeze(2).broadcast_to([128, GB, 3])

            def gate_products(i, bank):
                dve.wait_ge(g1_done, i)
                after(dve, g2_done, i - 1)
                dve.scalar_tensor_tensor(out=gprod[:, :, :], in0=per_batch(bank[:, 0:GB]), scalar=0.0,
                                         in1=g2_sb[:, :].unsqueeze(1).broadcast_to([128, GB, 3]),
                                         op0=ALU.max, op1=ALU.mult).then_inc(gprod_ready, 1)

            def gate_max(i, bank):
                dve.wait_ge(g2_done, i)
                logits = bank[:, 0:GB * 3].rearrange("p (b k) -> p b k", b=GB)
                dve.tensor_reduce(gmax[:, :], logits, AX.X, ALU.max).then_inc(gmax_ready, 1)
                dve.wait_ge(gmax_ready, i)
                dve.tensor_tensor(gsub[:, :, :], logits, per_batch(gmax[:, :]), ALU.subtract).then_inc(gsub_ready, 1)

            def gate_sum(i):
                dve.wait_ge(gexp_ready, i)
                dve.tensor_reduce(gsum[:, :], gexp[:, :, :], AX.X, ALU.add).then_inc(gate_steps, 1)

            def gate_reciprocal(i):
                dve.wait_ge(gate_steps, i * 3 - 2)
                dve.reciprocal(grec[:, :], gsum[:, :]).then_inc(gate_steps, 1)

            def gate_scale(i):
                dve.wait_ge(gate_steps, i * 3 - 1)
                dve.tensor_tensor(gate[:, :, :], gexp[:, :, :], per_batch(grec[:, :]), ALU.mult).then_inc(gate_steps, 1)

            def mix(part, p, n):
                if n == 0:
                    after(dve, z_done, part.free)
                else:
                    dve.wait_ge(mixed, part.n * 3 - 3 + n)
                src = x1T[:, p] if n == 0 else x2T[:, :]
                for b in part.batches:
                    op = dve.scalar_tensor_tensor(out=cols(x2T, b), in0=cols(acc_sb[:, p, (2, 0, 1)[n]], b),
                                                  scalar=gate[:, b, n:n + 1], in1=cols(src, b), op0=ALU.mult, op1=ALU.add)
                op.then_inc(mixed, 1)

            def y_sum(part, bank):
                dve.wait_ge(y_done, part.n)
                dve.wait_ge(x2b_ready, part.n)
                after(dve, yg_ready, part.free)
                dve.tensor_tensor(y[:, part.cols], bank[:, part.cols], x2b[:, part.cols], ALU.add).then_inc(y_ready, 1)

            def y_stats(part, batches):
                dve.wait_ge(y_ready, part.n)
                after(dve, meanvar_ready, part.free)
                for b in batches:
                    op = dve.bn_stats(stats[:, b, :], cols(y, b))
                    if b == part.batches[-1]:
                        op.then_inc(stats_ready, 1)

            def y_meanvar(part):
                for b in part.batches:
                    op = dve.bn_aggr(meanvar[:, b, :], stats[:, b, :])
                op.then_inc(meanvar_ready, 1)

            def centered(part, b):
                op = dve.scalar_tensor_tensor(out=cols(yg, b), in0=cols(y, b), scalar=meanvar[:, b, 0:1],
                                              in1=g_sel[:, b, :], op0=ALU.subtract, op1=ALU.mult)
                if b == part.batches[-1]:
                    op.then_inc(yg_ready, 1)

            def ln_wait(part, k):
                if part is LAST[1]:
                    dve.wait_ge(ln_steps_last, k)
                else:
                    dve.wait_ge(ln_steps, part.n * LN_STEPS - LN_STEPS + k)

            def ln_step(part, k):
                if k > 0:
                    ln_wait(part, k)
                v, h, r = var[:, part.small], half[:, part.small], rstd[:, part.small]
                square, scaled = nt[:, 0, part.small], nt[:, 1, part.small]
                if k == 0:
                    op = dve.tensor_scalar(v, meanvar[:, part.small, 1], EPS, None, ALU.add)
                elif k == 1:
                    op = dve.tensor_scalar(h, v.bitcast(I32), 1, None, ALU.arith_shift_right)
                elif k == 2:
                    op = dve.tensor_scalar(r.bitcast(I32), h, -1.0, RSQRT_MAGIC, ALU.mult, ALU.add)
                elif k % 3 == 0:
                    op = dve.tensor_tensor(square, r, r, ALU.mult)
                elif k % 3 == 1:
                    op = dve.scalar_tensor_tensor(out=scaled, in0=square, scalar=-0.5, in1=v, op0=ALU.mult, op1=ALU.mult)
                else:
                    op = dve.scalar_tensor_tensor(out=r, in0=scaled, scalar=1.5, in1=r, op0=ALU.add, op1=ALU.mult)
                op.then_inc(ln_steps_last if part is LAST[1] else ln_steps, 1)

            def newton(part, r):
                for k in range(3 * r + 3, 3 * r + 6):
                    ln_step(part, k)

            def x3_waits(part):
                ln_wait(part, LN_STEPS)
                dve.wait_ge(yg_ready, part.n)
                dve.wait_ge(x2nb_ready, part.n)
                used = part.free + HEAD
                if part.banks:
                    used = used - 1
                after(dve, x3t_done, used)
                after(dve, o_ready, used)

            def x3_batch(part, b):
                op = dve.scalar_tensor_tensor(out=cols(x3[:, part.parity], b), in0=cols(yg, b), scalar=rstd[:, b:b + 1],
                                              in1=cols(x2nb, b), op0=ALU.mult, op1=ALU.add)
                if b == part.batches[-1]:
                    op.then_inc(x3_ready, 1)

            def queries(part, bank):
                dve.wait_ge(x3t_done, part.n + HEAD)
                dve.wait_ge(em_sel_ready, part.n)
                dve.tensor_tensor(qT[:, part.cols], bank[:, part.cols], em_sel[:, :, :].rearrange("p b n -> p (b n)")[:, part.cols],
                                  ALU.add).then_inc(qt_ready, 1)

            def maxima(part, bank, lo=None, hi=None):
                lo, hi = part.small.start if lo is None else lo, part.small.stop if hi is None else hi
                dve.wait_ge(qk_done, part.n + HEAD)
                op = dve.tensor_reduce(negmax[:, lo:hi], bank[:, lo * 128:hi * 128].rearrange("p (b n) -> p b n", n=128),
                                       AX.X, ALU.max, negate=True)
                if hi == part.small.stop:
                    op.then_inc(negmax_ready, 1)

            def row_sums(part):
                dve.wait_ge(probs_ready, part.n)
                dve.reciprocal(prec[:, part.small], psums[:, part.small]).then_inc(prec_ready, 1)

            def result(part, bank, batches=None):
                dve.wait_ge(pv_done, part.n + HEAD)
                dve.wait_ge(prec_ready, part.n + HEAD)
                after(dve, stored, (part.free - (1 if part.banks else 0)) * 16 + 16 * HEAD)
                dve.wait_ge(x3_ready, part.n + HEAD)
                for b in batches or part.batches:
                    op = dve.scalar_tensor_tensor(out=cols(o_sb[:, part.parity], b), in0=cols(bank, b), scalar=prec[:, b:b + 1],
                                                  in1=cols(x3[:, part.parity], b), op0=ALU.mult, op1=ALU.add)
                    if b == part.batches[-1]:
                        op.then_inc(o_ready, 1)

            def slot(s):
                i, p = s.i, s.p
                l2, l3 = Part(i, 1 - p), Part(i - 1, p)

                def relu_lo(k):
                    n = (shared_until(k) - 1) % 4
                    dve.wait_ge(hi_ready, i * UNITS + k + 1)
                    dve.scalar_tensor_tensor(out=hid_lo[:, n], in0=hid_ps[k % 3][:, :], scalar=0.0,
                                             in1=hid_hi[:, n].bitcast(F32), op0=ALU.max, op1=ALU.subtract).then_inc(lo_ready, 1)

                for t in range(UNITS):
                    if s.mlp and is_shared(t) and not (t == 10 and s.prev):
                        relu_lo(t)
                    if isinstance(i, int) and i == 0 and t < 2:
                        table_lo(2 + t)
                    if t == 0 and s.attn:
                        newton(l3, 0)
                        newton(l3, 1)
                    if t == 1 and s.attn:
                        newton(l3, 2)
                        gate_products(i, misc[0])
                        x3_waits(l3)
                        for b in l3.batches:
                            x3_batch(l3, b)
                    if t == 2 and s.prev and not s.attn:
                        gate_products(i, misc[0])
                    if t == 3 and s.prev:
                        gate_max(i, misc[1])
                    if t == 4 and s.prev:
                        gate_sum(i)
                    if t == 4 and s.attn:
                        queries(l3, misc[0])
                    if t == 4 and s.prev:
                        gate_reciprocal(i)
                        gate_scale(i)
                        dve.wait_ge(gate_steps, i * 3)
                        dve.wait_ge(acc_ready, i * 3)
                        mix(l2, 1 - p, 0)
                    if t == 5 and s.attn:
                        maxima(l3, misc[1])
                    if t == 5 and s.prev:
                        mix(l2, 1 - p, 1)
                    if t == 6 and s.prev:
                        mix(l2, 1 - p, 2)
                    if t == 6 and s.prep:
                        if s.prev:
                            dve.wait_ge(mixed, i * 3 - 2)
                        dve.wait_ge(l0_done, i + 2)
                        dve.wait_ge(b0_sel_ready, i + 2)
                        for b in range(GB):
                            op = dve.scalar_tensor_tensor(out=cols(x1T[:, 1 - p], b), in0=cols(misc[0], b),
                                                          scalar=b0_sel[:, b:b + 1], in1=cols(xT, b), op0=ALU.add, op1=ALU.add)
                            if isinstance(i, int) and i == -1 and b == GB // 2 - 1:
                                op.then_inc(x1_half_ready, 1)
                        op.then_inc(x1_ready, 1)
                        if isinstance(i, int) and i == -1:
                            for done, part in ((x1h_half_ready, slice(0, W // 2)), (x1h_ready, slice(W // 2, W))):
                                dve.wait_ge(done, 1)
                                op = dve.tensor_tensor(x1l[:, 0, part], x1T[:, 0, part], x1h[:, 0, part].bitcast(F32), ALU.subtract)
                            op.then_inc(x1l_ready, 1)
                            table_lo(1)
                    if t == 8 and s.attn:
                        row_sums(l3)
                    if t == 10 and s.prev:
                        y_sum(l2, misc[0])
                        y_stats(l2, l2.batches)
                        dve.wait_ge(stats_ready, i)
                        relu_lo(t)
                        y_meanvar(l2)
                    if t == 11 and s.prev:
                        dve.wait_ge(g_sel_ready, i)
                        if s.attn:
                            dve.wait_ge(x3_ready, i - 1 + HEAD)
                        dve.wait_ge(meanvar_ready, i)
                        for b in range(GB):
                            if b < 3:
                                ln_step(l2, b)
                            centered(l2, b)
                    if t == 11 and s.attn:
                        result(l3, misc[1])

            def tail():
                before, (first, second), (_, third, fourth) = Part(NG - 1, 0), LAST, LAST_L3
                newton(before, 0)
                newton(before, 1)
                gate_products(NG, GATE_BANKS[0])
                newton(before, 2)
                gate_max(NG, GATE_BANKS[1])
                x3_waits(before)
                x3_batch(before, 0)
                x3_batch(before, 1)
                gate_sum(NG)
                gate_reciprocal(NG)
                gate_scale(NG)
                dve.wait_ge(gate_steps, NG * 3)
                dve.wait_ge(acc_ready, NG * 3)
                for n in range(3):
                    mix(first, 1, n)
                x3_batch(before, 2)
                x3_batch(before, 3)
                queries(before, misc[0])
                dve.wait_ge(g_sel_ready, NG)
                dve.wait_ge(x3_ready, NG - 1 + HEAD)
                y_sum(first, first.bank("Y"))
                y_stats(first, first.batches)
                dve.wait_ge(stats_ready, first.n)
                y_meanvar(first)
                dve.wait_ge(meanvar_ready, first.n)
                ln_step(first, 0)
                centered(first, 0)
                ln_step(first, 1)
                centered(first, 1)
                ln_step(first, 2)
                maxima(before, misc[1], 0, 2)
                ln_step(first, 3)
                maxima(before, misc[1], 2, 4)
                ln_step(first, 4)
                y_sum(second, second.bank("Y"))
                ln_step(first, 5)
                y_stats(second, [2])
                ln_step(first, 6)
                y_stats(second, [3])
                ln_step(first, 7)
                ln_step(first, 8)
                dve.wait_ge(stats_ready, second.n)
                y_meanvar(second)
                ln_step(first, 9)
                dve.wait_ge(meanvar_ready, second.n)
                ln_step(second, 0)
                ln_step(first, 10)
                ln_step(second, 1)
                ln_step(first, 11)
                centered(second, 2)
                x3_waits(first)
                x3_batch(first, 0)
                ln_step(second, 2)
                x3_batch(first, 1)
                ln_step(second, 3)
                centered(second, 3)
                ln_step(second, 4)
                queries(first, first.bank("X3T"))
                ln_step(second, 5)
                row_sums(before)
                ln_step(second, 6)
                result(before, misc[1], [0])
                ln_step(second, 7)
                maxima(first, first.bank("QK"))
                ln_step(second, 8)
                ln_step(second, 9)
                result(before, misc[1], [1])
                ln_step(second, 10)
                ln_step(second, 11)
                x3_waits(second)
                x3_batch(third, 2)
                x3_batch(fourth, 3)
                result(before, misc[1], [2])
                queries(third, third.bank("X3T"))
                queries(fourth, fourth.bank("X3T"))
                result(before, misc[1], [3])
                maxima(third, third.bank("QK"))
                maxima(fourth, fourth.bank("QK"))
                row_sums(first)
                result(first, first.bank("PV"))
                row_sums(third)
                row_sums(fourth)
                result(third, third.bank("PV"))
                result(fourth, fourth.bank("PV"))

            run_slots(dve, slot, tail=tail)

        @block.gpsimd
        def _(pool):
            pool.memset(ones[:, :], 1.0).then_inc(consts, 1)
            pool.memset(ident[:, :], 0.0).then_inc(consts, 1)
            pool.wait_ge(consts, 2)
            pool.affine_select(out=ident[:, :], in_=ident[:, :], compare_op=ALU.not_equal, fill=1.0,
                               base=0, pattern=[[-1, 128]], channel_multiplier=1).then_inc(consts, 1)
            pool.iota(row_i[:, :], [[0, 1]], base=0, channel_multiplier=1).then_inc(consts, 1)
            pool.wait_ge(cols_ready, 1)

            def bd_columns(i):
                after(pool, zt_ready, i - 1)
                pool.tensor_copy(bd_sel[:, :], columns[:, 1, bass.ds(i * GB - GB, GB)]).then_inc(bd_sel_ready, 1)

            def table_rows(i):
                who = [pool.value_load(ids[0:1, 2, bass.ds(i * GB - GB + b, 1)], min_val=0, max_val=P2 - 1) for b in range(GB)]
                token = [pool.value_load(ids[0:1, 3, bass.ds(i * GB - GB + b, 1)], min_val=0, max_val=P3 - 1) for b in range(GB)]
                return [[ln_table[:, m, bass.ds(w_, 1), :].rearrange("p s d -> p (s d)") for w_ in who] for m in range(3)] + [
                    [em_table[:, bass.ds(t_, 1), :].rearrange("p s d -> p (s d)") for t_ in token]]

            def g_rows(i, ln_g_):
                after(pool, yg_ready, i - 1)
                for b in range(GB):
                    op = pool.tensor_copy(g_sel[:, b, :], ln_g_[b])
                op.then_inc(g_sel_ready, 1)

            def x2_bias(part, up_b_):
                pool.wait_ge(x2n_ready, part.n)
                after(pool, y_ready, part.free)
                for b in part.batches:
                    op = pool.tensor_tensor(cols(x2b, b), cols(x2n, b), up_b_[b], ALU.add)
                op.then_inc(x2b_ready, 1)

            def x2_ln_bias(part, ln_b_):
                after(pool, x3_ready, part.free + HEAD)
                for b in part.batches:
                    op = pool.tensor_tensor(cols(x2nb, b), cols(x2n, b), ln_b_[b], ALU.add)
                op.then_inc(x2nb_ready, 1)

            def embeddings(part, embed_):
                after(pool, qt_ready, part.free)
                for b in part.batches:
                    op = pool.tensor_copy(em_sel[:, b, :], embed_[b])
                op.then_inc(em_sel_ready, 1)

            def slot(s):
                i, p = s.i, s.p
                l2 = Part(i, 1 - p)
                if s.prep:
                    after(pool, x1_ready, i + 1)
                    pool.tensor_copy(b0_sel[:, :], columns[:, 0, bass.ds((i * GB + GB) % B, GB)]).then_inc(b0_sel_ready, 1)
                if s.prev:
                    bd_columns(i)
                    if isinstance(i, int) and i == 1:
                        pool.wait_ge(ids_in, 48)
                        pool.wait_ge(lntab_in, 64)
                    up_b_, ln_g_, ln_b_, embed_ = table_rows(i)
                    g_rows(i, ln_g_)
                if s.prep and not (isinstance(i, int) and i == -1):
                    pool.wait_ge(x1h_ready, i + 2)
                    pool.tensor_tensor(x1l[:, 1 - p], x1T[:, 1 - p], x1h[:, 1 - p].bitcast(F32),
                                       ALU.subtract).then_inc(x1l_ready, 1)
                if s.prev:
                    x2_bias(l2, up_b_)
                    x2_ln_bias(l2, ln_b_)
                    embeddings(l2, embed_)

            def tail():
                (first, second), (_, third, fourth) = LAST, LAST_L3
                bd_columns(NG)
                up_b_, ln_g_, ln_b_, embed_ = table_rows(NG)
                g_rows(NG, ln_g_)
                for n in range(3):
                    pool.wait_ge(scaled_ready, n + 1)
                    after(pool, mixed_last, n)
                    pool.tensor_tensor(x2T[:, second.cols], (x1T[:, 1] if n == 0 else x2T)[:, second.cols], scaled[:, n],
                                       ALU.add).then_inc(mixed_last, 1)
                x2_bias(first, up_b_)
                x2_bias(second, up_b_)
                x2_ln_bias(first, ln_b_)
                x2_ln_bias(second, ln_b_)
                embeddings(first, embed_)
                embeddings(third, embed_)
                embeddings(fourth, embed_)

            run_slots(pool, slot, tail=tail)


_INS = ["x", "itok_B_0_7", "itok_B_0_2", "itok_B_0_6", "fside_BxSxS_0", "itok_B_0_5",
        "L0_cond_weight", "L0_cond_bias", "L1_cond_wi", "L1_cond_wo", "L1_cond_swi", "L1_cond_swo",
        "L1_cond_g1", "L1_cond_g2", "L2_cond_down_w", "L2_cond_down_b", "L2_cond_up_w", "L2_cond_up_b",
        "L2_cond_ln_g", "L2_cond_ln_b", "L3_cond_braak_embed"]


def kernel(**inputs):
    import numpy as _np
    import concourse.bacc as _bacc
    from concourse import mybir as _mybir
    from concourse.bass_utils import run_bass_kernel_spmd as _run

    nc = _bacc.Bacc("TRN2", target_bir_lowering=False, num_devices=1)
    arrays, args = {}, []
    for name in _INS:
        a = _np.ascontiguousarray(inputs[name])
        arrays[f"in_{name}_dram"] = a
        args.append(nc.dram_tensor(f"in_{name}_dram", a.shape, _mybir.dt.from_np(a.dtype), kind="ExternalInput").ap())
    shape = inputs["x"].shape
    args.append(nc.dram_tensor("out_0_dram", shape, _mybir.dt.float32, kind="ExternalOutput").ap())
    build(nc, *args)
    r = _run(nc, [arrays], core_ids=[0])
    return r.results[0]["out_0_dram"]
```
